# Optimizing a Trainium2 kernel written in Bass

```python
import numpy as np
import jax
import jax.numpy as jnp

def _softmax(x, axis=-1):
    return jax.nn.softmax(x, axis=axis)

def _gelu(x):
    return jax.nn.gelu(x, approximate=True)

def _silu(x):
    return jax.nn.silu(x)

def _sigmoid(x):
    return jax.nn.sigmoid(x)

def _layernorm(x, axis=-1, eps=1e-05):
    m = jnp.mean(x, axis=axis, keepdims=True)
    v = jnp.var(x, axis=axis, keepdims=True)
    return (x - m) / jnp.sqrt(v + eps)

def _scatter_add(tgt, idx, src, axis=0):
    return tgt.at[idx].add(src)

def _segment_sum(src, seg, n):
    return jax.ops.segment_sum(src, seg, n)
kernel_name = 'mk_cond_seq_d2_seqx_r8_6e26a4'

def setup_inputs(seed: int=0):
    np.random.seed(seed)
    _w = jnp.asarray

    def _rec_inputs():
        import jax
        import jax.numpy as jnp
        _rk = jax.random.key(seed)
        x = 1.648e-05 + 1 * jax.random.normal(jax.random.fold_in(_rk, 1), (32, 32, 144), jnp.float32)
        _lenS = 32 - jax.random.randint(jax.random.fold_in(_rk, 7), (32,), 0, max(1, 32 // 4) + 1, jnp.int32)
        _lenS2 = 32 - jax.random.randint(jax.random.fold_in(_rk, 8), (32,), 0, max(1, 32 // 4) + 1, jnp.int32)
        cond_1152 = 0.00914911 + 1.00357 * jax.random.normal(jax.random.fold_in(_rk, 11), (32, 144), jnp.float32)
        return (x, cond_1152)
    x, cond_1152 = _rec_inputs()

    def _L0_cond_setup():
        import jax, jax.numpy as jnp
        import numpy as np
        HID = 144
        HEADS = 16
        HD = HID // HEADS
        MLP = int(HID * 4.0)

        def _ln(x, eps, gamma=None, beta=None):
            mu = jnp.mean(x, axis=-1, keepdims=True)
            var = jnp.mean(jnp.square(x - mu), axis=-1, keepdims=True)
            y = (x - mu) / jnp.sqrt(var + eps)
            if gamma is not None:
                y = y * gamma + beta
            return y
        key = jax.random.key(seed)
        ks = jax.random.split(key, 12)
        B, N, C = (8, 128, HID)
        s = lambda k, *sh: jax.random.normal(k, sh, dtype=jnp.float32) * 0.02
        return {'x': jax.random.normal(ks[0], (B, N, C), dtype=jnp.float32), 'c': jax.random.normal(ks[1], (B, C), dtype=jnp.float32), 'w_qkv': s(ks[2], C, 3 * C), 'b_qkv': jnp.zeros((3 * C,), jnp.float32), 'w_proj': s(ks[3], C, C), 'b_proj': jnp.zeros((C,), jnp.float32), 'qn_g': jnp.ones((HD,), jnp.float32), 'qn_b': jnp.zeros((HD,), jnp.float32), 'kn_g': jnp.ones((HD,), jnp.float32), 'kn_b': jnp.zeros((HD,), jnp.float32), 'w1': s(ks[4], C, MLP), 'b1': jnp.zeros((MLP,), jnp.float32), 'w2': s(ks[5], MLP, C), 'b2': jnp.zeros((C,), jnp.float32), 'w_ada': s(ks[6], C, 6 * C), 'b_ada': jnp.zeros((6 * C,), jnp.float32)}
    _L0_cond_all = _L0_cond_setup()
    _L0_cond_in = {k: v for k, v in _L0_cond_all.items() if k in ('w_qkv', 'b_qkv', 'w_proj', 'b_proj', 'qn_g', 'qn_b', 'kn_g', 'kn_b', 'w1', 'b1', 'w2', 'b2', 'w_ada', 'b_ada')}
    del _L0_cond_all

    def _L1_cond_setup():
        import jax, jax.numpy as jnp
        import numpy as np
        B, T, D, H = (64, 32, 144, 16)
        HD = D // H
        EPS = 1e-06

        def _ln(x):
            mu = jnp.mean(x, axis=-1, keepdims=True)
            var = jnp.var(x, axis=-1, keepdims=True)
            return (x - mu) * jax.lax.rsqrt(var + EPS)

        def _modulate(x, shift, scale):
            return x * (1.0 + scale[:, None, :]) + shift[:, None, :]

        def _attn(x, Wq, Wk, Wv, Wp, bp):
            b, t, d = x.shape
            q = (x @ Wq).reshape(b, t, H, HD).transpose(0, 2, 1, 3)
            k = (x @ Wk).reshape(b, t, H, HD).transpose(0, 2, 1, 3)
            v = (x @ Wv).reshape(b, t, H, HD).transpose(0, 2, 1, 3)
            scores = jnp.einsum('bhqd,bhkd->bhqk', q, k) / np.sqrt(HD)
            mask = jnp.triu(jnp.ones((t, t), bool), k=1)
            scores = jnp.where(mask, -jnp.inf, scores)
            w = jax.nn.softmax(scores, axis=-1)
            ctx = jnp.einsum('bhqk,bhkd->bhqd', w, v).transpose(0, 2, 1, 3).reshape(b, t, d)
            return ctx @ Wp + bp

        def _mlp(x, W1, b1, W2, b2):
            return jax.nn.silu(x @ W1 + b1) @ W2 + b2
        key = jax.random.key(seed)
        ks = jax.random.split(key, 12)
        s = lambda fan_in: 1.0 / np.sqrt(fan_in)
        return {'x': jax.random.normal(ks[0], (B, T, D), jnp.float32), 'c': jax.random.normal(ks[1], (B, D), jnp.float32), 'Wq': jax.random.normal(ks[2], (D, D), jnp.float32) * s(D), 'Wk': jax.random.normal(ks[3], (D, D), jnp.float32) * s(D), 'Wv': jax.random.normal(ks[4], (D, D), jnp.float32) * s(D), 'Wp': jax.random.normal(ks[5], (D, D), jnp.float32) * s(D), 'bp': jnp.zeros((D,), jnp.float32), 'W1': jax.random.normal(ks[6], (D, 4 * D), jnp.float32) * s(D), 'b1': jnp.zeros((4 * D,), jnp.float32), 'W2': jax.random.normal(ks[7], (4 * D, D), jnp.float32) * s(4 * D), 'b2': jnp.zeros((D,), jnp.float32), 'Wa': jax.random.normal(ks[8], (D, 6 * D), jnp.float32) * s(D), 'ba': jnp.zeros((6 * D,), jnp.float32)}
    _L1_cond_all = _L1_cond_setup()
    _L1_cond_in = {k: v for k, v in _L1_cond_all.items() if k in ('Wq', 'Wk', 'Wv', 'Wp', 'bp', 'W1', 'b1', 'W2', 'b2', 'Wa', 'ba')}
    del _L1_cond_all
    return {'x': x, 'cond_1152': cond_1152, 'L0_cond_w_qkv': _L0_cond_in['w_qkv'], 'L0_cond_b_qkv': _L0_cond_in['b_qkv'], 'L0_cond_w_proj': _L0_cond_in['w_proj'], 'L0_cond_b_proj': _L0_cond_in['b_proj'], 'L0_cond_qn_g': _L0_cond_in['qn_g'], 'L0_cond_qn_b': _L0_cond_in['qn_b'], 'L0_cond_kn_g': _L0_cond_in['kn_g'], 'L0_cond_kn_b': _L0_cond_in['kn_b'], 'L0_cond_w1': _L0_cond_in['w1'], 'L0_cond_b1': _L0_cond_in['b1'], 'L0_cond_w2': _L0_cond_in['w2'], 'L0_cond_b2': _L0_cond_in['b2'], 'L0_cond_w_ada': _L0_cond_in['w_ada'], 'L0_cond_b_ada': _L0_cond_in['b_ada'], 'L1_cond_Wq': _L1_cond_in['Wq'], 'L1_cond_Wk': _L1_cond_in['Wk'], 'L1_cond_Wv': _L1_cond_in['Wv'], 'L1_cond_Wp': _L1_cond_in['Wp'], 'L1_cond_bp': _L1_cond_in['bp'], 'L1_cond_W1': _L1_cond_in['W1'], 'L1_cond_b1': _L1_cond_in['b1'], 'L1_cond_W2': _L1_cond_in['W2'], 'L1_cond_b2': _L1_cond_in['b2'], 'L1_cond_Wa': _L1_cond_in['Wa'], 'L1_cond_ba': _L1_cond_in['ba']}

def reference(x, cond_1152, L0_cond_w_qkv, L0_cond_b_qkv, L0_cond_w_proj, L0_cond_b_proj, L0_cond_qn_g, L0_cond_qn_b, L0_cond_kn_g, L0_cond_kn_b, L0_cond_w1, L0_cond_b1, L0_cond_w2, L0_cond_b2, L0_cond_w_ada, L0_cond_b_ada, L1_cond_Wq, L1_cond_Wk, L1_cond_Wv, L1_cond_Wp, L1_cond_bp, L1_cond_W1, L1_cond_b1, L1_cond_W2, L1_cond_b2, L1_cond_Wa, L1_cond_ba):
    import jax
    import jax.numpy as jnp

    def _L0_cond_ref(x, c, w_qkv, b_qkv, w_proj, b_proj, qn_g, qn_b, kn_g, kn_b, w1, b1, w2, b2, w_ada, b_ada):
        import jax, jax.numpy as jnp
        import numpy as np
        HID = 144
        HEADS = 16
        HD = HID // HEADS
        MLP = int(HID * 4.0)

        def _ln(x, eps, gamma=None, beta=None):
            mu = jnp.mean(x, axis=-1, keepdims=True)
            var = jnp.mean(jnp.square(x - mu), axis=-1, keepdims=True)
            y = (x - mu) / jnp.sqrt(var + eps)
            if gamma is not None:
                y = y * gamma + beta
            return y
        B, N, C = x.shape
        H, hd = (HEADS, HD)
        scale = hd ** (-0.5)
        mod = jax.nn.silu(c) @ w_ada + b_ada
        sh_msa, sc_msa, g_msa, sh_mlp, sc_mlp, g_mlp = jnp.split(mod, 6, axis=1)
        xn = _ln(x, 1e-06)
        xn = xn * (1 + sc_msa[:, None, :]) + sh_msa[:, None, :]
        qkv = (xn @ w_qkv + b_qkv).reshape(B, N, 3, H, hd)
        q, k, v = (qkv[:, :, 0], qkv[:, :, 1], qkv[:, :, 2])
        q = _ln(q, 1e-05, qn_g, qn_b)
        k = _ln(k, 1e-05, kn_g, kn_b)
        attn = jnp.einsum('bqhd,bkhd->bhqk', q, k) * scale
        attn = jax.nn.softmax(attn, axis=-1)
        o = jnp.einsum('bhqk,bkhd->bqhd', attn, v).reshape(B, N, C)
        o = o @ w_proj + b_proj
        x = x + g_msa[:, None, :] * o
        xn2 = _ln(x, 1e-06)
        xn2 = xn2 * (1 + sc_mlp[:, None, :]) + sh_mlp[:, None, :]
        h = jax.nn.gelu(xn2 @ w1 + b1, approximate=False)
        m = h @ w2 + b2
        x = x + g_mlp[:, None, :] * m
        return x

    def _L1_cond_ref(x, c, Wq, Wk, Wv, Wp, bp, W1, b1, W2, b2, Wa, ba):
        import jax, jax.numpy as jnp
        import numpy as np
        B, T, D, H = (64, 32, 144, 16)
        HD = D // H
        EPS = 1e-06

        def _ln(x):
            mu = jnp.mean(x, axis=-1, keepdims=True)
            var = jnp.var(x, axis=-1, keepdims=True)
            return (x - mu) * jax.lax.rsqrt(var + EPS)

        def _modulate(x, shift, scale):
            return x * (1.0 + scale[:, None, :]) + shift[:, None, :]

        def _attn(x, Wq, Wk, Wv, Wp, bp):
            b, t, d = x.shape
            q = (x @ Wq).reshape(b, t, H, HD).transpose(0, 2, 1, 3)
            k = (x @ Wk).reshape(b, t, H, HD).transpose(0, 2, 1, 3)
            v = (x @ Wv).reshape(b, t, H, HD).transpose(0, 2, 1, 3)
            scores = jnp.einsum('bhqd,bhkd->bhqk', q, k) / np.sqrt(HD)
            mask = jnp.triu(jnp.ones((t, t), bool), k=1)
            scores = jnp.where(mask, -jnp.inf, scores)
            w = jax.nn.softmax(scores, axis=-1)
            ctx = jnp.einsum('bhqk,bhkd->bhqd', w, v).transpose(0, 2, 1, 3).reshape(b, t, d)
            return ctx @ Wp + bp

        def _mlp(x, W1, b1, W2, b2):
            return jax.nn.silu(x @ W1 + b1) @ W2 + b2
        mod = jax.nn.silu(c) @ Wa + ba
        sh_msa, sc_msa, g_msa, sh_mlp, sc_mlp, g_mlp = jnp.split(mod, 6, axis=1)
        x = x + g_msa[:, None, :] * _attn(_modulate(_ln(x), sh_msa, sc_msa), Wq, Wk, Wv, Wp, bp)
        x = x + g_mlp[:, None, :] * _mlp(_modulate(_ln(x), sh_mlp, sc_mlp), W1, b1, W2, b2)
        return x
    x = _L0_cond_ref(x, cond_1152, L0_cond_w_qkv, L0_cond_b_qkv, L0_cond_w_proj, L0_cond_b_proj, L0_cond_qn_g, L0_cond_qn_b, L0_cond_kn_g, L0_cond_kn_b, L0_cond_w1, L0_cond_b1, L0_cond_w2, L0_cond_b2, L0_cond_w_ada, L0_cond_b_ada)
    x = _L1_cond_ref(x, cond_1152, L1_cond_Wq, L1_cond_Wk, L1_cond_Wv, L1_cond_Wp, L1_cond_bp, L1_cond_W1, L1_cond_b1, L1_cond_W2, L1_cond_b2, L1_cond_Wa, L1_cond_ba)
    return x

_drawn_inputs = setup_inputs


def setup_inputs(seed=0):
    import zlib

    import numpy as np

    out = dict(_drawn_inputs(seed))
    spreads = {'L0_cond_b_qkv': (0.0, 0.8),
     'L0_cond_b_proj': (0.0, 0.413),
     'L0_cond_qn_g': (1.0, 0.6),
     'L0_cond_qn_b': (0.0, 0.8),
     'L0_cond_kn_g': (1.0, 0.6),
     'L0_cond_kn_b': (0.0, 2.0),
     'L0_cond_b1': (0.0, 0.8),
     'L0_cond_b2': (0.0, 0.403),
     'L0_cond_b_ada': (0.0, 0.441),
     'L1_cond_bp': (0.0, 0.297),
     'L1_cond_b1': (0.0, 0.482),
     'L1_cond_b2': (0.0, 0.301),
     'L1_cond_ba': (0.0, 0.1)}
    factors = {'L0_cond_w_qkv': 8.0, 'L0_cond_w_proj': 8.0, 'L0_cond_w1': 5.231, 'L0_cond_w2': 4.825}
    for name, (base, spread) in spreads.items():
        noise = np.random.default_rng([zlib.crc32(name.encode()), seed]).standard_normal(out[name].shape)
        drawn = base * np.exp(spread * noise) if base else spread * noise
        out[name] = jnp.asarray(drawn.astype(out[name].dtype))
    for name, factor in factors.items():
        out[name] = (out[name] * factor).astype(out[name].dtype)
    return out
```

```python
from contextlib import ExitStack

import concourse.bass as bass
from concourse import mybir

F32 = mybir.dt.float32
BF16 = mybir.dt.bfloat16
I32 = mybir.dt.int32
ALU = mybir.AluOpType
ACT = mybir.ActivationFunctionType
AX = mybir.AxisListType.X

B, N, C = 32, 32, 144
H, HD = 16, 9
F = 4 * C
P = 128
SEQ = P // N
T = B // SEQ
CH = C // 2
KH = [CH, CH + 1]
Q3 = 3 * C
M6 = 6 * C
QG, HG = 4, 2
SETS = H // (QG * HG)
GH = 4
G = H // GH
VW = HD + 1
FM = (F + P - 1) // P
FR = F - (FM - 1) * P
CT = 2
CW = CT * P
CHUNKS = T // CT
EPS_X, EPS_QK = 1e-6, 1e-5
MAGIC = float(0x5F3759DF)
NEWTON = 3
RS_OPS = 1 + 4 * NEWTON
MASKED = -1e30


def build(nc, x_d, c_d, w_d, const_d, mask_d, out_d):
    with ExitStack() as ctx:
        def sb(name, shape, dt=F32):
            return ctx.enter_context(nc.sbuf_tensor(name, shape, dt))

        def bank(name):
            return ctx.enter_context(nc.psum_tensor(name, [P, 512], F32))

        def sem(name):
            return ctx.enter_context(nc.semaphore(name))

        x = sb("x", [P, T, C])
        ident = sb("ident", [P, P])
        ident_bf = sb("ident_bf", [P, P], BF16)
        mask_f = sb("mask_f", [P, N])
        mask_bf = sb("mask_bf", [P, N], BF16)
        head_cols = sb("head_cols", [P, HG + 1])
        wqkv = [sb(f"wqkv{l}", [CH + 1, 2, Q3]) for l in range(2)]
        wproj = [sb(f"wproj{l}", [CH + 1, 2, C]) for l in range(2)]
        w1 = [sb(f"w1_{l}", [CH + 1, 2, F]) for l in range(2)]
        w2 = [sb(f"w2_{l}", [P, FM, C]) for l in range(2)]
        wada = [sb(f"wada{l}", [CH + 1, 2, M6]) for l in range(2)]
        head_mean = sb("head_mean", [CH + 1, 2, 2 * H])
        cond = sb("cond", [B, C])
        cond_t = sb("cond_t", [CH + 1, 2, B])
        mod = sb("mod", [B, 2, M6])
        modb = [sb(f"modb{l}", [P, T, M6]) for l in range(2)]
        qk_gain = sb("qk_gain", [P, 2, 2])
        q_aff = sb("q_aff", [P, 2, 2])
        k_aff = sb("k_aff", [P, 2, HG, 2])
        stats = sb("stats", [P, CT, 6])
        mv = sb("mv", [P, CT, 2])
        ln_rs = sb("ln_rs", [P, CT])
        ln_t = sb("ln_t", [P, 2, CT])
        xc = sb("xc", [P, C])
        xn = sb("xn", [P, CT, C])
        xt = sb("xt", [CH + 1, 2, P])
        xt2 = sb("xt2", [CH + 1, 2, CW])
        v = sb("v", [P, T, C])
        vblk = sb("vblk", [P, SEQ, G, GH, VW])
        sq = sb("sq", [P, 2 * C])
        ssum = sb("ssum", [P, 2 * H])
        qk_rs = sb("qk_rs", [P, 2 * H])
        qk_t = sb("qk_t", [P, 2, 2 * H])
        qkn = sb("qkn", [P, 2 * SETS * QG, N])
        qt = sb("qt", [P, SETS, P])
        kblk = sb("kblk", [P, SETS, HG, P])
        smax = sb("smax", [P, H])
        prob = sb("prob", [P, H, N])
        prob_t = sb("prob_t", [P, G, P])
        srec = sb("srec", [P, H])
        o = sb("o", [P, C])
        ot = sb("ot", [CH + 1, 2, P])
        y = sb("y", [P, CT, C])
        ht = sb("ht", [P, FM, CW])

        ps_t = bank("ps_t")
        ps_q = bank("ps_q")
        ps_s = ctx.enter_context(nc.psum_tensor("ps_s", [P, QG, 512], F32))
        ps_pt, ps_o = bank("ps_pt"), bank("ps_o")
        ps_h = [ps_q, ps_s[:, 0, :], ps_s[:, 1, :], ps_s[:, 2, :], ps_s[:, 3, :]]
        ps_y = [ps_o, ps_pt]

        s_ident, s_const, s_cond, s_x, s_qkg = sem("s_ident"), sem("s_const"), sem("s_cond"), sem("s_x"), sem("s_qkg")
        s_wada = [sem("s_wada0"), sem("s_wada1")]
        s_w = [sem("s_w0"), sem("s_w1")]
        s_set = sem("s_set")
        s_setc = sem("s_setc")
        s_zero = sem("s_zero")
        s_silu, s_ct, s_ctc, s_mod, s_mods = sem("s_silu"), sem("s_ct"), sem("s_ctc"), sem("s_mod"), sem("s_mods")
        s_modd, s_modb = [sem("s_modd0"), sem("s_modd1")], [sem("s_modb0"), sem("s_modb1")]
        s_lnc = sem("s_lnc")
        s_lnv = sem("s_lnv")
        s_lnr = sem("s_lnr")
        s_pool = sem("s_pool")
        s_xn, s_xnt, s_xt, s_qkv, s_sq = sem("s_xn"), sem("s_xnt"), sem("s_xt"), sem("s_qkv"), sem("s_sq")
        s_v, s_vblk, s_ssum, s_qkr = sem("s_v"), sem("s_vblk"), sem("s_ssum"), sem("s_qkr")
        s_qkn, s_qkt, s_qt, s_kblk = sem("s_qkn"), sem("s_qkt"), sem("s_qt"), sem("s_kblk")
        s_s, s_max, s_sub, s_exp, s_pt, s_ptc = sem("s_s"), sem("s_max"), sem("s_sub"), sem("s_exp"), sem("s_pt"), sem("s_ptc")
        s_o, s_rec, s_on, s_ott, s_ot, s_proj = sem("s_o"), sem("s_rec"), sem("s_on"), sem("s_ott"), sem("s_ot"), sem("s_proj")
        s_gate, s_res = sem("s_gate"), sem("s_res")
        s_xn2, s_x2t, s_xt2, s_h, s_ht = sem("s_xn2"), sem("s_x2t"), sem("s_xt2"), sem("s_h"), sem("s_ht")
        s_y, s_gate2, s_res2, s_out = sem("s_y"), sem("s_gate2"), sem("s_res2"), sem("s_out")

        scratch = nc.dram_tensor("mod_scratch", (2, B, M6), F32).ap()

        def seg(l, part, t):
            return modb[l][:, t, part * C:(part + 1) * C]

        def pipeline(eng, step, first, last):
            for n in range(first, 1):
                step(n)
            with eng.Fori(1, T - 2) as n:
                step(n)
            for n in range(T - 2, last + 1):
                step(n)

        def at(n, first, last):
            return not isinstance(n, int) or first <= n <= last

        block = ctx.enter_context(nc.Block())

        @block.sync
        def _(sp):
            sp.dma_start(cond[:], c_d).then_inc(s_cond, 16)
            sp.dma_start(ident[:], const_d[:, 0:P]).then_inc(s_ident, 16)
            for l in range(2):
                wa, ba = w_d[l][8:10]
                sp.dma_start(wada[l][0:CH], wa.rearrange("(h p) m -> p h m", p=CH)).then_inc(s_wada[l], 16)
                sp.dma_start(wada[l][CH:CH + 1, 1], ba.rearrange("(a m) -> a m", a=1)).then_inc(s_wada[l], 16)
                if l == 0:
                    sp.dma_start(head_cols[:], const_d[:, P:P + HG + 1]).then_inc(s_const, 16)
                    sp.dma_start(mask_f[:], mask_d).then_inc(s_const, 16)
            for l in range(2):
                sp.wait_ge(s_mods, 2 * (l + 1))
                sp.dma_start(scratch[l], mod[:, l, :]).then_inc(s_modd[l], 16)
            for l in range(2):
                sp.wait_ge(s_modd[l], 16)
                for part in (slice(0, 2 * C), slice(2 * C, 3 * C), slice(3 * C, M6)):
                    for j in range(SEQ):
                        src = scratch[l, j::SEQ, part].rearrange("(a t) m -> a t m", a=1).broadcast_to(
                            [N, T, part.stop - part.start])
                        sp.dma_start(modb[l][N * j:N * j + N, :, part], src).then_inc(s_modb[l], 16)
            for t in range(T):
                if t % CT == 0:
                    sp.wait_ge(s_res2, T + t + CT)
                sp.dma_start(out_d[t], x[:, t, :]).then_inc(s_out, 16)
            sp.wait_ge(s_out, 16 * T)

        @block.gpsimd
        def _(pool):
            links = [0]

            def link(ins):
                links[0] += 1
                ins.then_inc(s_pool, 1)
                pool.wait_ge(s_pool, links[0])

            gp = nc.gpsimd
            gp.memset(cond_t[:], 1.0).then_inc(s_zero, 1)
            gp.memset(xt[:], 1.0).then_inc(s_zero, 1)
            gp.memset(xt2[:], 1.0).then_inc(s_zero, 1)
            gp.memset(ot[:], 1.0).then_inc(s_zero, 1)
            gp.memset(ht[:, FM - 1, :], 1.0).then_inc(s_zero, 1)
            gp.memset(qkn[:], 0.0).then_inc(s_zero, 1)
            gp.memset(vblk[:], 0.0).then_inc(s_zero, 1)
            pool.wait_ge(s_zero, 7)
            for h in range(GH):
                gp.memset(vblk[N * h:N * h + N, :, :, h, HD:VW], 1.0).then_inc(s_zero, 1)
            pool.wait_ge(s_zero, 7 + GH)

            def build_vblk(g, t):
                pool.wait_ge(s_v, g + 1)
                if not (isinstance(t, int) and g == 0):
                    pool.wait_ge(s_o, g)
                for h in range(GH):
                    for j in range(SEQ):
                        last = gp.tensor_copy(
                            vblk[N * h:N * h + N, j, :, h, 0:HD],
                            v[N * j:N * j + N, bass.ds(t, 1), :].rearrange("p a (s g h c) -> p (a s) g h c", s=SETS, g=G, h=HG)
                            [:, h // HG, :, h % HG, :])
                last.then_inc(s_vblk, 1)

            for l in range(2):
                def step(n, l=l):
                    if at(n + 1, 0, T - 1):
                        build_vblk(T * l + n + 1, n + 1)
                pipeline(pool, step, -1, T - 2)

        @block.scalar
        def _(act):
            a = nc.scalar
            for l in range(2):
                if l == 0:
                    for i, (gain, bias) in enumerate(((w_d[0][10], w_d[0][11]), (w_d[0][12], w_d[0][13]))):
                        act.wait_ge(s_setc, 1)
                        for grp in range(QG):
                            for h in range(HG):
                                r = N * grp + HD * h
                                act.dma_start(qk_gain[r:r + HD, i, 0:1], gain.rearrange("(c a) -> c a", a=1)).then_inc(s_qkg, 16)
                                act.dma_start(qk_gain[r:r + HD, i, 1:2], bias.rearrange("(c a) -> c a", a=1)).then_inc(s_qkg, 16)
                wq, bq, wp, bp, wa1, b1, wa2, b2 = w_d[l][:8]
                act.dma_start(wqkv[l][0:CH], wq if l else wq.rearrange("(h p) m -> p h m", p=CH)).then_inc(s_w[l], 16) if l == 0 else None
                if l == 1:
                    for i in range(3):
                        act.dma_start(wqkv[1][0:CH, :, i * C:(i + 1) * C], wq[i].rearrange("(h p) m -> p h m", p=CH)).then_inc(s_w[1], 16)
                else:
                    act.dma_start(wqkv[0][CH:CH + 1, 1], bq.rearrange("(a m) -> a m", a=1)).then_inc(s_w[0], 16)
                    act.dma_start(x[:], x_d).then_inc(s_x, 16)
                for i in range(QG):
                    r = i % 2 * (CH // 2)
                    act.dma_start(wproj[l][r:r + CH // 2, i // 2],
                                  wp.rearrange("(s i r) m -> s i r m", s=SETS, i=QG)[:, i]).then_inc(s_w[l], 16)
                act.dma_start(w1[l][0:CH], wa1.rearrange("(h p) m -> p h m", p=CH)).then_inc(s_w[l], 16)
                for dst, b in ((wproj, bp), (w1, b1)):
                    act.dma_start(dst[l][CH:CH + 1, 1], b.rearrange("(a m) -> a m", a=1)).then_inc(s_w[l], 16)
                act.dma_start(w2[l][:, 0:FM - 1], wa2[0:(FM - 1) * P].rearrange("(k p) m -> p k m", p=P)).then_inc(s_w[l], 16)
                act.dma_start(w2[l][0:FR, FM - 1], wa2[(FM - 1) * P:F]).then_inc(s_w[l], 16)
                act.dma_start(w2[l][FR:FR + 1, FM - 1], b2.rearrange("(a m) -> a m", a=1)).then_inc(s_w[l], 16)

            act.wait_ge(s_cond, 16)
            a.activation(cond[:], cond[:], ACT.Silu).then_inc(s_silu, 1)

            def step(n, l):
                g = T * l + n
                if at(n + 1, 0, T - 1):
                    act.wait_ge(s_xnt, g + 2)
                    a.copy(xt[0:CH], ps_t[0:CH, 0:2 * P].rearrange("p (h t) -> p h t", h=2)).then_inc(s_xt, 1)
                if at(n - 1, 0, T - 1):
                    act.wait_ge(s_pt, g)
                    a.copy(prob_t[:], ps_pt[:].rearrange("p (g t) -> p g t", g=G)).then_inc(s_ptc, 1)
                if at(n + 1, 0, T - 1):
                    act.wait_ge(s_qkv, g + 2)
                    if not (isinstance(n, int) and g < 0):
                        act.wait_ge(s_qkn, g + 1)
                    if l == 0:
                        a.activation(sq[:], ps_q[:, 0:2 * C], ACT.Square).then_inc(s_sq, 1)
                    a.copy(v[:, bass.ds(n + 1, 1), :], ps_q[:, 2 * C:3 * C].unsqueeze(1)).then_inc(s_v, 1)
                if at(n - 1, 0, T - 1):
                    act.wait_ge(s_ott, g)
                    a.copy(ot[0:CH], ps_t[0:CH, 0:2 * P].rearrange("p (h t) -> p h t", h=2)).then_inc(s_ot, 1)
                if at(n + 1, 0, T - 1):
                    act.wait_ge(s_qkt, g + 2)
                    if not (isinstance(n, int) and g < 0):
                        act.wait_ge(s_s, g + 1)
                    a.activation(qt[:], ps_q[:, 0:SETS * P].rearrange("p (s t) -> p s t", s=SETS), ACT.Identity,
                                 scale=q_aff[:, l, 0:1], bias=q_aff[:, l, 1:2]).then_inc(s_qt, 1)
                if at(n, 0, T - 1):
                    act.wait_ge(s_sub, g + 1)
                    a.activation(prob[:], prob[:], ACT.Exp).then_inc(s_exp, 1)

            def mlp(l, c, transposes_next):
                u = CHUNKS * l + c
                for m in range(FM):
                    rows = P if m < FM - 1 else FR
                    act.wait_ge(s_h, FM * u + m + 1)
                    if m == 0 and not (isinstance(c, int) and u == 0):
                        act.wait_ge(s_y, CT * u)
                    a.activation(ht[0:rows, m, :], ps_h[m][0:rows, 0:CW], ACT.Silu if l else ACT.Gelu).then_inc(s_ht, 1)
                if transposes_next:
                    evac_xt2(u + 1)

            def evac_xt2(u):
                act.wait_ge(s_x2t, u + 1)
                a.copy(xt2[0:CH], ps_t[0:CH, :].rearrange("p (h t) -> p h t", h=2)).then_inc(s_xt2, 1)

            act.wait_ge(s_zero, 11)
            act.wait_ge(s_ct, 1)
            a.copy(cond_t[0:CH], ps_t[0:CH, 0:2 * B].rearrange("p (h t) -> p h t", h=2)).then_inc(s_ctc, 1)
            act.wait_ge(s_set, 1)
            for l in range(2):
                pipeline(act, lambda n, l=l: step(n, l), -1, T)
                evac_xt2(CHUNKS * l)
                mlp(l, 0, True)
                with act.Fori(1, CHUNKS - 1) as c:
                    mlp(l, c, True)
                mlp(l, CHUNKS - 1, False)

        @block.vector
        def _(dve):
            d = nc.vector
            setup = [0]

            def link(ins):
                setup[0] += 1
                ins.then_inc(s_setc, 1)
                dve.wait_ge(s_setc, setup[0])

            link(d.memset(qk_gain[:], 0.0))
            for l in range(2):
                for half in range(2):
                    dve.wait_ge(s_mod, 2 * l + half + 1)
                    base = half * 3 * C
                    ps = ps_h[2 * l + half]
                    link(d.tensor_copy(mod[:, l, base:base + 3 * C], ps[0:B, 0:3 * C]))
                    d.tensor_scalar(mod[:, l, base + C:base + 2 * C], ps[0:B, C:2 * C], 1.0, None, ALU.add).then_inc(s_mods, 1)
            dve.wait_ge(s_ident, 16)
            dve.wait_ge(s_const, 16 * 2)
            link(d.tensor_copy(ident_bf[:], ident[:]))
            link(d.tensor_copy(mask_bf[:], mask_f[:]))
            dve.wait_ge(s_qkg, 16 * 2 * 2 * QG * HG)
            link(d.tensor_scalar(q_aff[:, 0, :], qk_gain[:, 0, :], HD ** -0.5, None, ALU.mult))
            link(d.memset(q_aff[:, 1, :], 0.0))
            link(d.memset(q_aff[:, 1, 0:1], HD ** -0.5))
            link(d.memset(k_aff[:, 1], 0.0))
            for h in range(HG):
                link(d.tensor_scalar(k_aff[:, 0, h, :], qk_gain[:, 1, :], head_cols[:, h:h + 1], None, ALU.mult))
                link(d.tensor_copy(k_aff[:, 1, h, 0:1], head_cols[:, h:h + 1]))
            dve.wait_ge(s_w[0], 16 * 12)
            for half in range(2):
                w = wqkv[0][0:KH[half], half, 0:2 * C].rearrange("p (g c) -> p g c", c=HD)
                hm = head_mean[0:KH[half], half, :]
                link(d.tensor_reduce(hm, w, AX, ALU.add))
                link(d.tensor_scalar(hm, hm, 1.0 / HD, None, ALU.mult))
                link(d.tensor_tensor(w, w, hm.unsqueeze(2).broadcast_to([KH[half], 2 * H, HD]), ALU.subtract))
            dve.wait_ge(s_zero, 11)
            d.memset(smax[:], 0.0).then_inc(s_set, 1)

            chain = {"ln": 0}

            def newton(rs, y_, t_, v_in, scale, eps, sem_c, c0):
                k = c0
                var, tmp = t_
                d.tensor_scalar(var, v_in, scale, eps, ALU.mult, ALU.add).then_inc(sem_c, 1)
                dve.wait_ge(sem_c, k + 1)
                d.tensor_scalar(rs.bitcast(I32), var.bitcast(I32), -0.5, MAGIC, ALU.mult, ALU.add).then_inc(sem_c, 1)
                k = k + 2
                for _ in range(NEWTON):
                    dve.wait_ge(sem_c, k)
                    d.scalar_tensor_tensor(tmp, rs, -0.5, rs, ALU.mult, ALU.mult).then_inc(sem_c, 1)
                    dve.wait_ge(sem_c, k + 1)
                    d.tensor_tensor(tmp, tmp, var, ALU.mult).then_inc(sem_c, 1)
                    dve.wait_ge(sem_c, k + 2)
                    d.scalar_tensor_tensor(rs, tmp, 1.5, rs, ALU.add, ALU.mult).then_inc(sem_c, 1)
                    k = k + 3
                dve.wait_ge(sem_c, k)

            NW = 2 + 3 * NEWTON
            LN_A = 2 + NW + 1
            LN_M = 2 * CT + NW + CT
            BLK = T * LN_A + CHUNKS * LN_M

            def layer_norm(l, first_tile, tiles, part, c0, done):
                for a_ in range(tiles):
                    d.bn_stats(stats[:, a_, :], x[:, bass.ds(first_tile + a_, 1), :]).then_inc(s_lnc, 1)
                for a_ in range(tiles):
                    dve.wait_ge(s_lnc, c0 + a_ + 1)
                    d.memset(ln_t[:, 0, a_:a_ + 1], 0.0)
                    d.bn_aggr(mv[:, a_, :], stats[:, a_, :]).then_inc(s_lnc, 1)
                dve.wait_ge(s_lnc, c0 + 2 * tiles)
                newton(ln_rs[:, 0:tiles], None, (ln_t[:, 0, 0:tiles], ln_t[:, 1, 0:tiles]), mv[:, 0:tiles, 1],
                       1.0, EPS_X, s_lnc, c0 + 2 * tiles)
                k = c0 + 2 * tiles + NW
                for a_ in range(tiles):
                    t = first_tile + a_
                    xv = x[:, bass.ds(t, 1), :].rearrange("p a c -> p (a c)")
                    shift = modb[l][:, bass.ds(t, 1), part * C:(part + 1) * C].rearrange("p a c -> p (a c)")
                    scale = modb[l][:, bass.ds(t, 1), (part + 1) * C:(part + 2) * C].rearrange("p a c -> p (a c)")
                    d.scalar_tensor_tensor(xn[:, a_, :], xv, mv[:, a_, 0:1], scale, ALU.subtract, ALU.mult).then_inc(s_lnc, 1)
                    dve.wait_ge(s_lnc, k + a_ + 1)
                    d.scalar_tensor_tensor(xn[:, a_, :], xn[:, a_, :], ln_rs[:, a_:a_ + 1], shift, ALU.mult, ALU.add)\
                     .then_inc(done, 1)

            QK_STEPS = NW

            def norm_qk(g, t):
                dve.wait_ge(s_sq, t + 1)
                d.tensor_reduce(ssum[:], sq[:].rearrange("p (g c) -> p g c", c=HD), AX, ALU.add).then_inc(s_ssum, 1)
                dve.wait_ge(s_ssum, (QK_STEPS + 1) * t + 1)
                newton(qk_rs[:], None, (qk_t[:, 0], qk_t[:, 1]), ssum[:], 1.0 / HD, EPS_QK, s_ssum, (QK_STEPS + 1) * t + 1)
                if not (isinstance(t, int) and t == 0):
                    dve.wait_ge(s_qkt, t)
                dve.wait_ge(s_v, t + 1)
                d.tensor_tensor(
                    qkn[:, :, 0:HG * HD].rearrange("p b (h c) -> p b h c", h=HG),
                    ps_q[:, 0:2 * C].rearrange("p (b h c) -> p b h c", h=HG, c=HD),
                    qk_rs[:].rearrange("p (b h) -> p b h", h=HG).unsqueeze(3).broadcast_to([P, 2 * SETS * QG, HG, HD]),
                    ALU.mult).then_inc(s_qkn, 1)

            def step(n, l):
                g = T * l + n
                if at(n + 1, 0, T - 1):
                    if l == 0:
                        norm_qk(g + 1, n + 1)
                    else:
                        dve.wait_ge(s_v, g + 2)
                        dve.wait_ge(s_qkt, g + 1)
                        d.tensor_copy(qkn[:, :, 0:HG * HD], ps_q[:, 0:2 * C].rearrange("p (b c) -> p b c", c=HG * HD))\
                         .then_inc(s_qkn, 1)
                if at(n - 1, 0, T - 1):
                    dve.wait_ge(s_o, g)
                    ov = ps_o[:, 0:H * VW].rearrange("p (h c) -> p h c", c=VW)
                    d.reciprocal(srec[:], ov[:, :, HD]).then_inc(s_rec, 1)
                    dve.wait_ge(s_rec, g)
                    if not (isinstance(n, int) and g <= 1):
                        dve.wait_ge(s_ott, g - 1)
                    d.tensor_tensor(o[:].rearrange("p (h c) -> p h c", c=HD), ov[:, :, 0:HD],
                                    srec[:].unsqueeze(2).broadcast_to([P, H, HD]), ALU.mult).then_inc(s_on, 1)
                if at(n + 2, 0, T - 1):
                    dve.wait_ge(s_xnt, g + 2)
                    layer_norm(l, n + 2, 1, 0, BLK * l + LN_A * (n + 2), s_xn)
                if at(n, 0, T - 1):
                    dve.wait_ge(s_s, g + 1)
                    sv = ps_s[:, :, 0:GH * N].rearrange("p g (h k) -> p g h k", k=N)
                    d.tensor_reduce(smax[:].rearrange("p (g h) -> p g h", g=G), sv, AX, ALU.max).then_inc(s_max, 1)
                    if not (isinstance(n, int) and g == 0):
                        dve.wait_ge(s_pt, g)
                    dve.wait_ge(s_max, g + 1)
                    d.tensor_tensor(prob[:].rearrange("p (g h) k -> p g h k", g=G), sv,
                                    smax[:].rearrange("p (g h) -> p g h", g=G).unsqueeze(3).broadcast_to([P, G, GH, N]),
                                    ALU.subtract).then_inc(s_sub, 1)
                if at(n + 1, 0, T - 1):
                    dve.wait_ge(s_qt, g + 2)
                    for h in range(HG):
                        last = d.tensor_scalar(kblk[:, :, h, :], ps_q[:, SETS * P:2 * SETS * P].rearrange("p (s t) -> p s t", s=SETS),
                                               k_aff[:, l, h, 0:1], k_aff[:, l, h, 1:2], ALU.mult, ALU.add)
                    last.then_inc(s_kblk, 1)
                if at(n - 1, 0, T - 1):
                    dve.wait_ge(s_proj, g)
                    residual(l, n - 1, g - 1, 2, ps_o, 0, s_gate, s_res)

            def residual(l, t, g, part, ps, slot, s_g, s_r):
                xv = x[:, bass.ds(t, 1), :].rearrange("p a c -> p (a c)")
                gate = modb[l][:, bass.ds(t, 1), part * C:(part + 1) * C].rearrange("p a c -> p (a c)")
                d.tensor_tensor(y[:, slot, :], ps[:, 0:C], gate, ALU.mult).then_inc(s_g, 1)
                dve.wait_ge(s_g, g + 1)
                d.tensor_tensor(xv, xv, y[:, slot, :], ALU.add).then_inc(s_r, 1)

            def mlp_norm(l, c):
                layer_norm(l, c * CT, CT, 3, BLK * l + T * LN_A + LN_M * c, s_xn2)

            def mlp_residual(l, c):
                u = CHUNKS * l + c
                for a_ in range(CT):
                    dve.wait_ge(s_y, CT * u + a_ + 1)
                    residual(l, CT * c + a_, CT * u + a_, 5, ps_y[a_], a_, s_gate2, s_res2)

            dve.wait_ge(s_x, 16)
            for l in range(2):
                dve.wait_ge(s_modb[l], 16 * 3 * SEQ)
                if l:
                    dve.wait_ge(s_res2, T * l)
                layer_norm(l, 0, 1, 0, BLK * l, s_xn)
                pipeline(dve, lambda n, l=l: step(n, l), -1, T)
                dve.wait_ge(s_res, T * (l + 1))
                dve.wait_ge(s_xnt, T * (l + 1))
                mlp_norm(l, 0)
                for c in range(1):
                    dve.wait_ge(s_x2t, CHUNKS * l + 1)
                    mlp_norm(l, 1)
                with dve.Fori(0, CHUNKS - 2) as c:
                    dve.wait_ge(s_x2t, CHUNKS * l + c + 2)
                    mlp_residual(l, c)
                    mlp_norm(l, c + 2)
                for c in range(CHUNKS - 2, CHUNKS):
                    mlp_residual(l, c)

        @block.tensor
        def _(pe):
            mm, tr = nc.tensor.matmul, nc.tensor.transpose
            pe.wait_ge(s_silu, 1)
            pe.wait_ge(s_ident, 16)
            for half in range(2):
                last = tr(ps_t[0:CH, half * B:half * B + B], cond[:, half * CH:half * CH + CH], ident[0:B, 0:B])
            last.then_inc(s_ct, 1)
            pe.wait_ge(s_ctc, 1)
            for l in range(2):
                pe.wait_ge(s_wada[l], 32)
                for part in range(2):
                    for half in range(2):
                        last = mm(ps_h[2 * l + part][0:B, 0:3 * C], cond_t[0:KH[half], half, :],
                                  wada[l][0:KH[half], half, part * 3 * C:(part + 1) * 3 * C], start=half == 0, stop=half == 1)
                    last.then_inc(s_mod, 1)
            pe.wait_ge(s_set, 1)

            def step(n, l):
                g = T * l + n
                if at(n + 1, 0, T - 1):
                    pe.wait_ge(s_xn, g + 2)
                    for half in range(2):
                        last = tr(ps_t[0:CH, half * P:half * P + P], xn[:, 0, half * CH:half * CH + CH], ident[:])
                    last.then_inc(s_xnt, 1)
                if at(n - 1, 0, T - 1):
                    pe.wait_ge(s_exp, g)
                    for grp in range(G):
                        last = tr(ps_pt[:, grp * P:grp * P + P], prob[:, grp * GH:(grp + 1) * GH, :].rearrange("p h k -> p (h k)"),
                                  ident[:])
                    last.then_inc(s_pt, 1)
                if at(n + 1, 0, T - 1):
                    pe.wait_ge(s_xt, g + 2)
                    if not (isinstance(n, int) and g < 0):
                        pe.wait_ge(s_kblk, g + 1)
                    rows = KH if l == 0 else [CH, CH]
                    for half in range(2):
                        last = mm(ps_q[:, 0:Q3], xt[0:rows[half], half, :], wqkv[l][0:rows[half], half, :],
                                  start=half == 0, stop=half == 1)
                    last.then_inc(s_qkv, 1)
                if at(n, 0, T - 1):
                    pe.wait_ge(s_qt, g + 1)
                    pe.wait_ge(s_kblk, g + 1)
                    if not (isinstance(n, int) and g == 0):
                        pe.wait_ge(s_sub, g)
                if at(n - 1, 0, T - 1):
                    pe.wait_ge(s_ptc, g)
                    pe.wait_ge(s_vblk, g)
                    if not (isinstance(n, int) and g <= 1):
                        pe.wait_ge(s_gate, g - 1)
                    for j in range(SEQ):
                        for grp in range(G):
                            vj = vblk[:, j, grp, :, :].rearrange("p h c -> p (h c)")
                            last = mm(ps_o[N * j:N * j + N, grp * GH * VW:(grp + 1) * GH * VW],
                                      prob_t[:, grp, N * j:N * j + N], vj, start=True, stop=True)
                    last.then_inc(s_o, 1)
                if at(n, 0, T - 1):
                    if l == 1:
                        for i in range(QG):
                            mm(ps_s[:, i, 0:GH * N], ident_bf[:], mask_bf[:].unsqueeze(1).broadcast_to([P, GH, N]),
                               start=True, stop=False, skip_group_check=True)
                    for s in range(SETS):
                        for j in range(SEQ):
                            for i in range(QG):
                                rows = slice(N * i, N * i + HG * HD)
                                last = mm(ps_s[N * j:N * j + N, i, s * HG * N:(s + 1) * HG * N], qt[rows, s, N * j:N * j + N],
                                          kblk[rows, s, :, N * j:N * j + N], start=l == 0, stop=True,
                                          skip_group_check=l == 1)
                    last.then_inc(s_s, 1)
                if at(n - 1, 0, T - 1):
                    pe.wait_ge(s_on, g)
                    for half in range(2):
                        last = tr(ps_t[0:CH, half * P:half * P + P], o[:, half * CH:half * CH + CH], ident[:])
                    last.then_inc(s_ott, 1)
                if at(n + 1, 0, T - 1):
                    pe.wait_ge(s_qkn, g + 2)
                    for k in range(2 * SETS):
                        last = tr(ps_q[:, k * P:k * P + P], qkn[:, k * QG:(k + 1) * QG, :].rearrange("p b c -> p (b c)"), ident[:])
                    last.then_inc(s_qkt, 1)
                if at(n - 1, 0, T - 1):
                    pe.wait_ge(s_ot, g)
                    for half in range(2):
                        last = mm(ps_o[:, 0:C], ot[0:KH[half], half, :], wproj[l][0:KH[half], half, :], start=half == 0, stop=half == 1)
                    last.then_inc(s_proj, 1)

            def mlp_transpose(l, c):
                u = CHUNKS * l + c
                pe.wait_ge(s_xn2, CT * (u + 1))
                for half in range(2):
                    for a_ in range(CT):
                        last = tr(ps_t[0:CH, half * CW + a_ * P:half * CW + (a_ + 1) * P], xn[:, a_, half * CH:half * CH + CH], ident[:])
                last.then_inc(s_x2t, 1)

            def mlp(l, c, transposes_next):
                u = CHUNKS * l + c
                pe.wait_ge(s_xt2, u + 1)
                for m in range(FM):
                    cols = P if m < FM - 1 else FR
                    for half in range(2):
                        last = mm(ps_h[m][0:cols, 0:CW], w1[l][0:KH[half], half, m * P:m * P + cols], xt2[0:KH[half], half, :],
                                  start=half == 0, stop=half == 1)
                    last.then_inc(s_h, 1)
                if transposes_next:
                    mlp_transpose(l, c + 1)
                pe.wait_ge(s_ht, FM * (u + 1))
                if not (isinstance(c, int) and c == 0):
                    pe.wait_ge(s_gate2, CT * u)
                for a_ in range(CT):
                    for m in range(FM):
                        rows = P if m < FM - 1 else FR + 1
                        last = mm(ps_y[a_][:, 0:C], ht[0:rows, m, a_ * P:(a_ + 1) * P], w2[l][0:rows, m, :], start=m == 0, stop=m == FM - 1)
                    last.then_inc(s_y, 1)

            for l in range(2):
                pe.wait_ge(s_w[l], 16 * (12 if l == 0 else 13))
                if l:
                    pe.wait_ge(s_res2, T * l)
                pipeline(pe, lambda n, l=l: step(n, l), -1, T)
                pe.wait_ge(s_res, T * (l + 1))
                mlp_transpose(l, 0)
                mlp(l, 0, True)
                with pe.Fori(1, CHUNKS - 1) as c:
                    mlp(l, c, True)
                mlp(l, CHUNKS - 1, False)


def kernel(**inputs):
    import numpy as np
    import concourse.bacc as bacc
    from concourse import mybir
    from concourse.bass_utils import run_bass_kernel_spmd

    nc = bacc.Bacc("TRN2", target_bir_lowering=False, num_devices=1)
    arrays = {}

    def given(name, a):
        a = np.ascontiguousarray(a)
        arrays["in_" + name] = a
        return nc.dram_tensor("in_" + name, a.shape, mybir.dt.from_np(a.dtype), kind="ExternalInput").ap()

    row = np.arange(P) % N
    heads = np.stack([(row // HD == h) for h in range(HG)] + [row < HG * HD], 1).astype(np.float32)
    const = given("const", np.concatenate([np.eye(P, dtype=np.float32), heads], 1))
    mask = given("mask", np.where(np.arange(N)[None, :] > (np.arange(P) % N)[:, None], np.float32(MASKED), np.float32(0)))
    x = given("x", inputs["x"]).rearrange("(t j) n c -> (j n) t c", j=SEQ)
    c = given("c", inputs["cond_1152"])
    w = [[given(k, inputs["L0_cond_" + k]) for k in
          ("w_qkv", "b_qkv", "w_proj", "b_proj", "w1", "b1", "w2", "b2", "w_ada", "b_ada", "qn_g", "qn_b", "kn_g", "kn_b")]]
    qkv1 = [given("L1_" + k, inputs["L1_cond_" + k]) for k in ("Wq", "Wk", "Wv")]
    w.append([qkv1, None] + [given("L1_" + k, inputs["L1_cond_" + k]) for k in ("Wp", "bp", "W1", "b1", "W2", "b2", "Wa", "ba")])
    out = nc.dram_tensor("out", (B, N, C), F32, kind="ExternalOutput").ap()
    build(nc, x, c, w, const, mask, out.rearrange("(t j) n c -> t (j n) c", j=SEQ))
    r = run_bass_kernel_spmd(nc, [arrays], core_ids=[0])
    return r.results[0]["out"]
```

```python
from contextlib import ExitStack

import concourse.bass as bass
from concourse import mybir

F32 = mybir.dt.float32
BF16 = mybir.dt.bfloat16
I32 = mybir.dt.int32
ALU = mybir.AluOpType
ACT = mybir.ActivationFunctionType
AX = mybir.AxisListType.X

B, N, C = 32, 32, 144
H, HD = 16, 9
F = 4 * C
P = 128
SEQ = P // N
T = B // SEQ
CH = C // 2
KR = CH + 1
KH = [CH, KR]
Q3 = 3 * C
M6 = 6 * C
QG, HG = 4, 2
SETS = H // (QG * HG)
GH = 4
G = H // GH
VW = HD + 1
FM = (F + P - 1) // P
FR = F - (FM - 1) * P
STEPS = range(-2, 2 * T + 3)
EPS_X, EPS_QK = 1e-6, 1e-5
MAGIC = float(0x5F3759DF)
RS_OPS = 8
RS_SCALE = 64 / 9
VQ, VX1, VX2 = slice(0, 2 * H), 2 * H, 2 * H + 1
VN = 2 * H + 2
MASKED = -1e30
ZERO = 9 + GH


def build(nc, x_d, c_d, const_d, w_d, out_d):
    with ExitStack() as ctx:
        def sb(name, shape, dt=F32):
            return ctx.enter_context(nc.sbuf_tensor(name, shape, dt))

        def bank(name):
            return ctx.enter_context(nc.psum_tensor(name, [P, 512], F32))

        def sem(name):
            return ctx.enter_context(nc.semaphore(name))

        const = sb("const", [P, P + N + 2 * HG + 4])
        ident = const[:, 0:P]
        mask_f = const[:, P:P + N]
        head_cols = const[:, P + N:P + N + HG]
        qk_gain = const[:, P + N + HG:P + N + HG + 4].rearrange("p (i b) -> p i b", i=2)
        ident_bf = sb("ident_bf", [P, P], BF16)
        mask_bf = sb("mask_bf", [P, N], BF16)
        wada = [sb(f"wada{l}", [KR, 2, M6]) for l in range(2)]
        wqkv = [sb(f"wqkv{l}", [P, 2, Q3]) for l in range(2)]
        wpw1 = [sb(f"wpw1_{l}", [P, 2, C + F]) for l in range(2)]
        w2 = [sb(f"w2_{l}", [P, FM, C]) for l in range(2)]
        head_mean = sb("head_mean", [P, 2, 2 * H])
        cond = sb("cond", [B, C])
        cond_t = sb("cond_t", [KR, 2, B])
        mod = sb("mod", [B, 2, M6])
        modb = [sb(f"modb{l}", [P, T, M6]) for l in range(2)]
        q_aff = sb("q_aff", [P, 2, 2])
        k_aff = sb("k_aff", [P, 2, HG, 2])
        x = sb("x", [P, T, C])
        stats = sb("stats", [P, 2, 6])
        mv = sb("mv", [P, 2, 2])
        var = sb("var", [P, VN])
        rs = sb("rs", [P, VN])
        rw = sb("rw", [P, 2, VN])
        xn = sb("xn", [P, C])
        xt = sb("xt", [P, 2, P])
        v = sb("v", [P, T, C])
        vblk = sb("vblk", [P, SEQ, G, GH, VW])
        sq = sb("sq", [P, 2 * C])
        ssum = sb("ssum", [P, 2 * H])
        qkn = sb("qkn", [P, 2 * SETS * QG, N])
        qt = sb("qt", [P, SETS, P])
        kblk = sb("kblk", [P, SETS, HG, P])
        smax = sb("smax", [P, H])
        prob = sb("prob", [P, H, N])
        prob_t = sb("prob_t", [P, G, P])
        srec = sb("srec", [P, H])
        o = sb("o", [P, C])
        ot = sb("ot", [P, 2, P])
        y = sb("y", [P, C])
        xn2 = sb("xn2", [P, C])
        xt2 = sb("xt2", [P, 2, P])
        ht = sb("ht", [P, FM, P])
        y2 = sb("y2", [P, C])

        ps_t = bank("ps_t")
        ps_q = bank("ps_q")
        ps_s = ctx.enter_context(nc.psum_tensor("ps_s", [P, QG, 512], F32))
        sv = ps_s[:, :, 0:GH * N]
        ps_pt = bank("ps_pt")
        ps_o = bank("ps_o")

        s_const, s_cond, s_x = sem("s_const"), sem("s_cond"), sem("s_x")
        s_wada = [sem("s_wada0"), sem("s_wada1")]
        s_wqkv = [sem("s_wqkv0"), sem("s_wqkv1")]
        s_w = [sem("s_w0"), sem("s_w1")]
        s_zero = sem("s_zero")
        s_chain = sem("s_chain")
        s_set = sem("s_set")
        s_cent = sem("s_cent")
        s_silu, s_ct, s_ctc, s_mod = sem("s_silu"), sem("s_ct"), sem("s_ctc"), sem("s_mod")
        s_mods = [sem("s_mods0"), sem("s_mods1")]
        s_modd = [sem("s_modd0"), sem("s_modd1")]
        s_modb = [[sem(f"s_modb{l}_{k}") for k in range(2)] for l in range(2)]
        s_bn1, s_bn2, s_mv1, s_mv2 = sem("s_bn1"), sem("s_bn2"), sem("s_mv1"), sem("s_mv2")
        s_ssum, s_vq = sem("s_ssum"), sem("s_vq")
        s_vx, s_rs = sem("s_vx"), sem("s_rs")
        s_xc1, s_xn, s_xnt, s_xt = sem("s_xc1"), sem("s_xn"), sem("s_xnt"), sem("s_xt")
        s_qkv, s_sq, s_v, s_vcopy, s_vblk = sem("s_qkv"), sem("s_sq"), sem("s_v"), sem("s_vcopy"), sem("s_vblk")
        s_qkn, s_qkt, s_qt, s_kblk = sem("s_qkn"), sem("s_qkt"), sem("s_qt"), sem("s_kblk")
        s_s, s_max, s_sub, s_exp = sem("s_s"), sem("s_max"), sem("s_sub"), sem("s_exp")
        s_pt, s_ptc, s_o, s_rec, s_on = sem("s_pt"), sem("s_ptc"), sem("s_o"), sem("s_rec"), sem("s_on")
        s_ott, s_ot, s_proj, s_gate, s_res = sem("s_ott"), sem("s_ot"), sem("s_proj"), sem("s_gate"), sem("s_res")
        s_xc2, s_xn2, s_x2t, s_xt2 = sem("s_xc2"), sem("s_xn2"), sem("s_x2t"), sem("s_xt2")
        s_h5, s_h, s_ht5, s_ht = sem("s_h5"), sem("s_h"), sem("s_ht5"), sem("s_ht")
        s_y, s_out = sem("s_y"), sem("s_out")
        s_gate2, s_res2 = sem("s_gate2"), sem("s_res2")

        scratch = nc.dram_tensor("mod_scratch", (2, B, M6), F32).ap()

        def pipeline(eng, step, ahead, behind):
            n = STEPS.start
            for l in range(2):
                for g in range(n, T * l + behind):
                    step(0, g)
                with eng.Fori(behind, T - ahead) as r:
                    step(l, r)
                n = T * (l + 1) - ahead
            for g in range(n, STEPS.stop):
                step(0, g)

        def pair(l, n, k):
            if isinstance(n, int):
                g = T * l + n + k
                return 0 <= g < 2 * T, g // T, g % T, g
            return True, l, n + k, T * l + n + k

        def wait_past(eng, s, count):
            if not isinstance(count, int) or count > 0:
                eng.wait_ge(s, count)

        def tile(buf, t, a=0, b=C):
            return buf[:, bass.ds(t, 1), a:b].rearrange("p a c -> p (a c)")

        block = ctx.enter_context(nc.Block())

        @block.sync
        def _(sp):
            sp.dma_start(cond[:], c_d).then_inc(s_cond, 16)
            sp.dma_start(const[:], const_d).then_inc(s_const, 16)
            sp.dma_start(wada[0][:], w_d[0][0]).then_inc(s_wada[0], 16)
            sp.dma_start(wqkv[0][:], w_d[0][1]).then_inc(s_wqkv[0], 16)
            sp.dma_start(x[:], x_d).then_inc(s_x, 16)
            sp.dma_start(wada[1][:], w_d[1][0]).then_inc(s_wada[1], 16)
            for l in range(2):
                sp.wait_ge(s_mods[l], 2)
                sp.dma_start(scratch[l], mod[:, l, :]).then_inc(s_modd[l], 16)
                if l == 0:
                    sp.dma_start(wpw1[0][:], w_d[0][2]).then_inc(s_w[0], 16)
                    sp.dma_start(w2[0][:], w_d[0][3]).then_inc(s_w[0], 16)
                sp.wait_ge(s_modd[l], 16)
                for k, part in enumerate((slice(0, 2 * C), slice(2 * C, M6))):
                    for j in range(SEQ):
                        src = scratch[l, j::SEQ, part].rearrange("(a t) m -> a t m", a=1).broadcast_to(
                            [N, T, part.stop - part.start])
                        sp.dma_start(modb[l][N * j:N * j + N, :, part], src).then_inc(s_modb[l][k], 16)
                if l == 0:
                    sp.dma_start(wqkv[1][:], w_d[1][1]).then_inc(s_wqkv[1], 16)
                    sp.dma_start(wpw1[1][:], w_d[1][2]).then_inc(s_w[1], 16)
                    sp.dma_start(w2[1][:], w_d[1][3]).then_inc(s_w[1], 16)
            for t in range(T):
                sp.wait_ge(s_res2, T + t + 2)
                sp.dma_start(out_d[t], x[:, t, :]).then_inc(s_out, 16)
            sp.wait_ge(s_out, 16 * T)

        @block.gpsimd
        def _(pool):
            gp = nc.gpsimd
            gp.memset(cond_t[:], 1.0).then_inc(s_zero, 1)
            gp.memset(xt[:], 1.0).then_inc(s_zero, 1)
            gp.memset(xt2[:], 1.0).then_inc(s_zero, 1)
            gp.memset(ot[:], 1.0).then_inc(s_zero, 1)
            gp.memset(ht[:, FM - 1, :], 1.0).then_inc(s_zero, 1)
            gp.memset(qkn[:], 0.0).then_inc(s_zero, 1)
            gp.memset(var[:], 1.0).then_inc(s_zero, 1)
            gp.memset(mv[:], 1.0).then_inc(s_zero, 1)
            gp.memset(vblk[:], 0.0).then_inc(s_zero, 1)
            pool.wait_ge(s_zero, 9)
            for h in range(GH):
                gp.memset(vblk[N * h:N * h + N, :, :, h, HD:VW], 1.0).then_inc(s_zero, 1)
            pool.wait_ge(s_zero, ZERO)
            gp.memset(y2[:], 0.0).then_inc(s_res2, 1)

            def step(l, n):
                ok, _, t, g = pair(l, n, 0)
                if ok:
                    pool.wait_ge(s_v, g + 1)
                    wait_past(pool, s_o, g)
                    for h in range(GH):
                        for j in range(SEQ):
                            last = gp.tensor_copy(
                                vblk[N * h:N * h + N, j, :, h, 0:HD],
                                v[N * j:N * j + N, bass.ds(t, 1), :].rearrange("p a (s g h c) -> p (a s) g h c", s=SETS, g=G, h=HG)
                                [:, h // HG, :, h % HG, :])
                        if h < GH - 1:
                            last.then_inc(s_vcopy, 1)
                            pool.wait_ge(s_vcopy, (GH - 1) * g + h + 1)
                    last.then_inc(s_vblk, 1)
                    pool.wait_ge(s_vblk, g + 1)
                ok, _, t, g = pair(l, n, -1)
                if ok:
                    pool.wait_ge(s_gate, g + 1)
                    gp.tensor_tensor(tile(x, t), tile(x, t), y[:], ALU.add).then_inc(s_res, 1)
                    pool.wait_ge(s_res, g + 1)
                ok, _, t, g = pair(l, n, -3)
                if ok:
                    pool.wait_ge(s_gate2, g + 2)
                    gp.tensor_tensor(tile(x, t), tile(x, t), y2[:], ALU.add).then_inc(s_res2, 1)
                    pool.wait_ge(s_res2, g + 2)

            pipeline(pool, step, 0, 3)

        @block.scalar
        def _(act):
            a = nc.scalar
            act.wait_ge(s_cond, 16)
            a.activation(cond[:], cond[:], ACT.Silu).then_inc(s_silu, 1)
            act.wait_ge(s_zero, ZERO)
            act.wait_ge(s_ct, 1)
            a.copy(cond_t[0:CH], ps_t[0:CH, 0:2 * B].rearrange("p (h t) -> p h t", h=2)).then_inc(s_ctc, 1)
            act.wait_ge(s_set, 1)

            def halves(ps):
                return ps[0:CH, 0:2 * P].rearrange("p (h t) -> p h t", h=2)

            def step(l, n):
                late, front, back, mlp = pair(l, n, 2), pair(l, n, 1), pair(l, n, -1), pair(l, n, -3)
                ok, b, t, g = back
                if ok:
                    act.wait_ge(s_sub, g + 1)
                    a.activation(prob[:], prob[:], ACT.Exp).then_inc(s_exp, 1)
                ok, b, t, g = front
                if ok:
                    act.wait_ge(s_qkv, g + 1)
                    if b == 0:
                        wait_past(act, s_vq, g)
                        a.activation(sq[:], ps_q[:, 0:2 * C], ACT.Square).then_inc(s_sq, 1)
                    a.copy(v[:, bass.ds(t, 1), :], ps_q[:, 2 * C:3 * C].unsqueeze(1)).then_inc(s_v, 1)
                ok, b, t, g = back
                if ok:
                    act.wait_ge(s_pt, g + 1)
                    a.copy(prob_t[:], ps_pt[:].rearrange("p (g t) -> p g t", g=G)).then_inc(s_ptc, 1)
                ok, b, t, g = mlp
                if ok:
                    func = ACT.Silu if b else ACT.Gelu
                    act.wait_ge(s_x2t, g + 1)
                    a.copy(xt2[0:CH], halves(ps_t)).then_inc(s_xt2, 1)
                    act.wait_ge(s_h5, g + 1)
                    a.activation(ht[0:FR, FM - 1, :], ps_pt[0:FR, 0:P], func).then_inc(s_ht5, 1)
                ok, b, t, g = back
                if ok:
                    act.wait_ge(s_ott, g + 1)
                    a.copy(ot[0:CH], halves(ps_t)).then_inc(s_ot, 1)
                ok, b, t, g = mlp
                if ok:
                    act.wait_ge(s_h, g + 1)
                    a.activation(ht[:, 0:FM - 1, :], sv, func).then_inc(s_ht, 1)
                ok, b, t, g = late
                if ok:
                    act.wait_ge(s_xnt, g + 1)
                    a.copy(xt[0:CH], halves(ps_t)).then_inc(s_xt, 1)
                ok, b, t, g = front
                if ok:
                    act.wait_ge(s_qkt, g + 1)
                    wait_past(act, s_s, g)
                    a.activation(qt[:], ps_pt[:, 0:SETS * P].rearrange("p (s t) -> p s t", s=SETS), ACT.Identity,
                                 scale=q_aff[:, b, 0:1], bias=q_aff[:, b, 1:2])
                    a.activation(kblk[:, :, 1, :], ps_pt[:, SETS * P:2 * SETS * P].rearrange("p (s t) -> p s t", s=SETS),
                                 ACT.Identity, scale=k_aff[:, b, 1, 0:1], bias=k_aff[:, b, 1, 1:2]).then_inc(s_qt, 1)

            pipeline(act, step, 2, 3)

        @block.vector
        def _(dve):
            d = nc.vector
            links = [0]

            def link(ins):
                links[0] += 1
                ins.then_inc(s_chain, 1)
                dve.wait_ge(s_chain, links[0])

            def modulation(l):
                for half in range(2):
                    dve.wait_ge(s_mod, 2 * l + half + 1)
                    base = half * 3 * C
                    ps = ps_s[0:B, 2 * l + half, 0:3 * C]
                    link(d.tensor_copy(mod[:, l, base:base + 3 * C], ps))
                    d.tensor_scalar(mod[:, l, base + C:base + 2 * C], ps[:, C:2 * C], 1.0, None, ALU.add).then_inc(s_mods[l], 1)

            dve.wait_ge(s_const, 16)
            link(d.tensor_copy(ident_bf[:], ident))
            link(d.tensor_copy(mask_bf[:], mask_f))
            link(d.tensor_scalar(q_aff[:, 0, :], qk_gain[:, 0, :], HD ** -0.5, None, ALU.mult))
            link(d.memset(q_aff[:, 1, :], 0.0))
            link(d.memset(q_aff[:, 1, 0:1], HD ** -0.5))
            link(d.memset(k_aff[:, 1], 0.0))
            for h in range(HG):
                link(d.tensor_scalar(k_aff[:, 0, h, :], qk_gain[:, 1, :], head_cols[:, h:h + 1], None, ALU.mult))
                link(d.tensor_copy(k_aff[:, 1, h, 0:1], head_cols[:, h:h + 1]))
            dve.wait_ge(s_zero, ZERO)
            d.memset(smax[:], 0.0).then_inc(s_set, 1)
            d.memset(rw[:], 0.0).then_inc(s_gate2, 1)
            modulation(0)
            dve.wait_ge(s_wqkv[0], 16)
            for half in range(2):
                w = wqkv[0][:, half, 0:2 * C].rearrange("p (g c) -> p g c", c=HD)
                hm = head_mean[:, half, :]
                link(d.tensor_reduce(hm, w, AX, ALU.add))
                link(d.tensor_scalar(hm, hm, 1.0 / HD, None, ALU.mult))
                d.tensor_tensor(w, w, hm.unsqueeze(2).broadcast_to([P, 2 * H, HD]), ALU.subtract).then_inc(s_cent, 1)

            def rsqrt(cols, s, base, first, stop):
                y, v, u, z = rs[:, cols], var[:, cols], rw[:, 0, cols], rw[:, 1, cols]
                for k in range(first, stop):
                    if k > 0:
                        dve.wait_ge(s, base + k)
                    if k == 0:
                        ins = d.tensor_scalar(y.bitcast(I32), v.bitcast(I32), -0.5, MAGIC, ALU.mult, ALU.add)
                    elif k == 1:
                        ins = d.tensor_tensor(u, y, y, ALU.mult)
                    elif k == 2 or k == 6:
                        ins = d.tensor_tensor(u, u, v, ALU.mult)
                    elif k == 3:
                        ins = d.scalar_tensor_tensor(u, u, -10 / 3, u, ALU.add, ALU.mult)
                    elif k == 4:
                        ins = d.scalar_tensor_tensor(z, u, 5.0, y, ALU.add, ALU.mult)
                    elif k == 5:
                        ins = d.scalar_tensor_tensor(u, z, -9 / 128, z, ALU.mult, ALU.mult)
                    else:
                        ins = d.scalar_tensor_tensor(y, u, 1.5, z, ALU.add, ALU.mult)
                    ins.then_inc(s, 1)

            def step(l, n):
                step_no = (T * l + n) - STEPS.start
                late, front, mid, back, prior, mlp = [pair(l, n, k) for k in (2, 1, 0, -1, -2, -3)]
                ok1, b1, t1, g1 = late
                ok2, b2, t2, g2 = prior
                if ok1:
                    if b1 == 1:
                        dve.wait_ge(s_res2, g1 - T + 2)
                    d.bn_stats(stats[:, 0, :], tile(x, t1)).then_inc(s_bn1, 1)
                if ok2:
                    dve.wait_ge(s_res, g2 + 1)
                    d.bn_stats(stats[:, 1, :], tile(x, t2)).then_inc(s_bn2, 1)
                if ok1:
                    dve.wait_ge(s_bn1, g1 + 1)
                if ok2:
                    dve.wait_ge(s_bn2, g2 + 1)
                if ok1 or ok2:
                    d.memset(rw[:, 0, VX1:VN], 0.0)
                if ok1:
                    d.bn_aggr(mv[:, 0, :], stats[:, 0, :]).then_inc(s_mv1, 1)
                if ok2:
                    d.bn_aggr(mv[:, 1, :], stats[:, 1, :]).then_inc(s_mv2, 1)
                if ok1:
                    dve.wait_ge(s_mv1, g1 + 1)
                if ok2:
                    dve.wait_ge(s_mv2, g2 + 1)
                if ok1 or ok2:
                    d.tensor_scalar(var[:, VX1:VN], mv[:, :, 1], EPS_X, RS_SCALE, ALU.add, ALU.mult).then_inc(s_vx, 1)
                ok, b, t, g = front
                norm = ok and b == 0
                if norm:
                    dve.wait_ge(s_sq, g + 1)
                    d.tensor_reduce(ssum[:], sq[:].rearrange("p (g c) -> p g c", c=HD), AX, ALU.add).then_inc(s_ssum, 1)
                    dve.wait_ge(s_ssum, g + 1)
                    d.tensor_scalar(var[:, VQ], ssum[:], RS_SCALE / HD, RS_SCALE * EPS_QK, ALU.mult, ALU.add).then_inc(s_vq, 1)
                    dve.wait_ge(s_vq, g + 1)
                roots = norm or ok1 or ok2
                root = slice(0 if norm else VX1, VN), s_rs, RS_OPS * step_no
                if ok1 or ok2:
                    dve.wait_ge(s_vx, step_no + 1)
                if roots:
                    rsqrt(*root, 0, 2)
                ok, b, t, g = mid
                s4 = sv.rearrange("p g (h k) -> p g h k", k=N)
                if ok:
                    dve.wait_ge(s_s, g + 1)
                    d.tensor_reduce(smax[:].rearrange("p (g h) -> p g h", g=G), s4, AX, ALU.max).then_inc(s_max, 1)
                if roots:
                    rsqrt(*root, 2, 3)
                if ok:
                    dve.wait_ge(s_max, g + 1)
                    wait_past(dve, s_pt, g)
                    d.tensor_tensor(prob[:].rearrange("p (g h) k -> p g h k", g=G), s4,
                                    smax[:].rearrange("p (g h) -> p g h", g=G).unsqueeze(3).broadcast_to([P, G, GH, N]),
                                    ALU.subtract).then_inc(s_sub, 1)
                if roots:
                    rsqrt(*root, 3, 4)
                ok, b, t, g = back
                ov = ps_o[:, 0:H * VW].rearrange("p (h c) -> p h c", c=VW)
                if ok:
                    dve.wait_ge(s_o, g + 1)
                    d.reciprocal(srec[:], ov[:, :, HD]).then_inc(s_rec, 1)
                if roots:
                    rsqrt(*root, 4, 5)
                if ok:
                    dve.wait_ge(s_rec, g + 1)
                    wait_past(dve, s_ott, g)
                    d.tensor_tensor(o[:].rearrange("p (h c) -> p h c", c=HD), ov[:, :, 0:HD],
                                    srec[:].unsqueeze(2).broadcast_to([P, H, HD]), ALU.mult).then_inc(s_on, 1)
                if roots:
                    rsqrt(*root, 5, 6)
                if ok1:
                    wait_past(dve, s_xnt, g1)
                    d.scalar_tensor_tensor(xn[:], tile(x, t1), mv[:, 0, 0:1], tile(modb[b1], t1, C, 2 * C),
                                           ALU.subtract, ALU.mult).then_inc(s_xc1, 1)
                if roots:
                    rsqrt(*root, 6, 7)
                if ok2:
                    wait_past(dve, s_x2t, g2)
                    d.scalar_tensor_tensor(xn2[:], tile(x, t2), mv[:, 1, 0:1], tile(modb[b2], t2, 4 * C, 5 * C),
                                           ALU.subtract, ALU.mult).then_inc(s_xc2, 1)
                if roots:
                    rsqrt(*root, 7, 8)
                    dve.wait_ge(s_rs, RS_OPS * (step_no + 1))
                if ok1:
                    dve.wait_ge(s_xc1, g1 + 1)
                    d.scalar_tensor_tensor(xn[:], xn[:], rs[:, VX1:VX1 + 1], tile(modb[b1], t1, 0, C),
                                           ALU.mult, ALU.add).then_inc(s_xn, 1)
                ok, b, t, g = front
                if ok:
                    dve.wait_ge(s_v, g + 1)
                    wait_past(dve, s_qkt, g)
                    if b == 0:
                        d.tensor_tensor(
                            qkn[:, :, 0:HG * HD].rearrange("p b (h c) -> p b h c", h=HG),
                            ps_q[:, 0:2 * C].rearrange("p (b h c) -> p b h c", h=HG, c=HD),
                            rs[:, VQ].rearrange("p (b h) -> p b h", h=HG).unsqueeze(3).broadcast_to([P, 2 * SETS * QG, HG, HD]),
                            ALU.mult).then_inc(s_qkn, 1)
                    else:
                        d.tensor_copy(qkn[:, :, 0:HG * HD], ps_q[:, 0:2 * C].rearrange("p (b c) -> p b c", c=HG * HD))\
                         .then_inc(s_qkn, 1)
                ok, b, t, g = back
                if ok:
                    dve.wait_ge(s_proj, g + 1)
                    wait_past(dve, s_res, g)
                    d.tensor_tensor(y[:], ps_o[:, 0:C], tile(modb[b], t, 2 * C, 3 * C), ALU.mult).then_inc(s_gate, 1)
                if ok2:
                    dve.wait_ge(s_xc2, g2 + 1)
                    d.scalar_tensor_tensor(xn2[:], xn2[:], rs[:, VX2:VX2 + 1], tile(modb[b2], t2, 3 * C, 4 * C),
                                           ALU.mult, ALU.add).then_inc(s_xn2, 1)
                ok, b, t, g = front
                if ok:
                    dve.wait_ge(s_qt, g + 1)
                    d.tensor_scalar(kblk[:, :, 0, :], ps_pt[:, SETS * P:2 * SETS * P].rearrange("p (s t) -> p s t", s=SETS),
                                    k_aff[:, b, 0, 0:1], k_aff[:, b, 0, 1:2], ALU.mult, ALU.add).then_inc(s_kblk, 1)
                ok, b, t, g = mlp
                if ok:
                    dve.wait_ge(s_y, g + 1)
                    dve.wait_ge(s_res2, g + 1)
                    d.tensor_tensor(y2[:], ps_o[:, 0:C], tile(modb[b], t, 5 * C, 6 * C), ALU.mult).then_inc(s_gate2, 1)

            modulation(1)
            dve.wait_ge(s_x, 16)
            def step_with_loads(l, n):
                if isinstance(n, int) and n == STEPS.start:
                    dve.wait_ge(s_modb[0][0], 16 * SEQ)
                if isinstance(n, int) and n == 1:
                    dve.wait_ge(s_modb[0][1], 16 * SEQ)
                if isinstance(n, int) and n == T - 2:
                    dve.wait_ge(s_modb[1][0], 16 * SEQ)
                    dve.wait_ge(s_modb[1][1], 16 * SEQ)
                step(l, n)

            pipeline(dve, step_with_loads, 2, 3)

        @block.tensor
        def _(pe):
            mm, tr = nc.tensor.matmul, nc.tensor.transpose

            def modulation(l):
                pe.wait_ge(s_wada[l], 16)
                for part in range(2):
                    for half in range(2):
                        last = mm(ps_s[0:B, 2 * l + part, 0:3 * C], cond_t[0:KH[half], half, :],
                                  wada[l][0:KH[half], half, part * 3 * C:(part + 1) * 3 * C], start=half == 0, stop=half == 1)
                    last.then_inc(s_mod, 1)

            def transpose_halves(src, done):
                for half in range(2):
                    last = tr(ps_t[0:CH, half * P:half * P + P], src[:, half * CH:half * CH + CH], ident)
                last.then_inc(done, 1)

            pe.wait_ge(s_silu, 1)
            pe.wait_ge(s_const, 16)
            for half in range(2):
                last = tr(ps_t[0:CH, half * B:half * B + B], cond[:, half * CH:half * CH + CH], ident[0:B, 0:B])
            last.then_inc(s_ct, 1)
            pe.wait_ge(s_ctc, 1)
            modulation(0)
            modulation(1)
            pe.wait_ge(s_mods[1], 2)
            pe.wait_ge(s_set, 1)
            pe.wait_ge(s_cent, 2)

            def step(l, n):
                if isinstance(n, int) and n == 1:
                    pe.wait_ge(s_w[0], 32)
                if isinstance(n, int) and n == T - 1:
                    pe.wait_ge(s_wqkv[1], 16)
                    pe.wait_ge(s_w[1], 32)
                late, front, mid, back, mlp = [pair(l, n, k) for k in (2, 1, 0, -1, -3)]
                ok, b, t, g = front
                if ok:
                    pe.wait_ge(s_xt, g + 1)
                    for half in range(2):
                        last = mm(ps_q[:, 0:Q3], xt[:, half, :], wqkv[b][:, half, :], start=half == 0, stop=half == 1)
                    last.then_inc(s_qkv, 1)
                ok, b, t, g = mid
                if ok:
                    pe.wait_ge(s_kblk, g + 1)
                ok, b, t, g = back
                if ok:
                    pe.wait_ge(s_exp, g + 1)
                    for grp in range(G):
                        last = tr(ps_pt[:, grp * P:grp * P + P], prob[:, grp * GH:(grp + 1) * GH, :].rearrange("p h k -> p (h k)"),
                                  ident)
                    last.then_inc(s_pt, 1)
                ok, b, t, g = mid
                if ok:
                    if b == 1:
                        for i in range(QG):
                            mm(ps_s[:, i, 0:GH * N], ident_bf[:], mask_bf[:].unsqueeze(1).broadcast_to([P, GH, N]),
                               start=True, stop=False, skip_group_check=True)
                    for s in range(SETS):
                        for j in range(SEQ):
                            for i in range(QG):
                                rows = slice(N * i, N * i + HG * HD)
                                last = mm(ps_s[N * j:N * j + N, i, s * HG * N:(s + 1) * HG * N], qt[rows, s, N * j:N * j + N],
                                          kblk[rows, s, :, N * j:N * j + N], start=b == 0, stop=True, skip_group_check=b == 1)
                    last.then_inc(s_s, 1)
                ok, b, t, g = mlp
                if ok:
                    pe.wait_ge(s_xn2, g + 1)
                    transpose_halves(xn2, s_x2t)
                ok, b, t, g = back
                if ok:
                    wait_past(pe, s_gate, g)
                    wait_past(pe, s_gate2, g - 1)
                    pe.wait_ge(s_vblk, g + 1)
                    pe.wait_ge(s_ptc, g + 1)
                    for j in range(SEQ):
                        for grp in range(G):
                            last = mm(ps_o[N * j:N * j + N, grp * GH * VW:(grp + 1) * GH * VW], prob_t[:, grp, N * j:N * j + N],
                                      vblk[:, j, grp, :, :].rearrange("p h c -> p (h c)"), start=True, stop=True)
                    last.then_inc(s_o, 1)

                def up(m):
                    cols = P if m < FM - 1 else FR
                    out = ps_s[:, m, 0:P] if m < FM - 1 else ps_pt[0:FR, 0:P]
                    for half in range(2):
                        last = mm(out, wpw1[b][:, half, C + m * P:C + m * P + cols], xt2[:, half, :], start=half == 0, stop=half == 1)
                    return last

                ok, b, t, g = mlp
                if ok:
                    pe.wait_ge(s_xt2, g + 1)
                    up(FM - 1).then_inc(s_h5, 1)
                    pe.wait_ge(s_sub, min(g + 4, 2 * T) if isinstance(n, int) else g + 4)
                    for m in range(FM // 2):
                        up(m)
                if back[0]:
                    pe.wait_ge(s_on, back[3] + 1)
                    transpose_halves(o, s_ott)
                if ok:
                    for m in range(FM // 2, FM - 1):
                        last = up(m)
                    last.then_inc(s_h, 1)
                ok, b, t, g = back
                if ok:
                    pe.wait_ge(s_ot, g + 1)
                    for half in range(2):
                        last = mm(ps_o[:, 0:C], ot[:, half, :], wpw1[b][:, half, 0:C], start=half == 0, stop=half == 1)
                    last.then_inc(s_proj, 1)
                ok, b, t, g = late
                if ok:
                    pe.wait_ge(s_xn, g + 1)
                    transpose_halves(xn, s_xnt)
                ok, b, t, g = front
                if ok:
                    if mlp[0]:
                        pe.wait_ge(s_ht5, g - 3)
                    pe.wait_ge(s_qkn, g + 1)
                    for k in range(2 * SETS):
                        last = tr(ps_pt[:, k * P:k * P + P], qkn[:, k * QG:(k + 1) * QG, :].rearrange("p b c -> p (b c)"), ident)
                    last.then_inc(s_qkt, 1)
                ok, b, t, g = mlp
                if ok:
                    pe.wait_ge(s_gate, min(g + 3, 2 * T) if isinstance(n, int) else g + 3)
                    if not back[0]:
                        pe.wait_ge(s_gate2, g + 1)
                    pe.wait_ge(s_ht, g + 1)
                    for m in range(FM):
                        rows = P if m < FM - 1 else FR + 1
                        last = mm(ps_o[:, 0:C], ht[0:rows, m, :], w2[b][0:rows, m, :], start=m == 0, stop=m == FM - 1)
                    last.then_inc(s_y, 1)

            pipeline(pe, step, 2, 3)


def kernel(**inputs):
    import numpy as np
    import concourse.bacc as bacc
    from concourse import mybir
    from concourse.bass_utils import run_bass_kernel_spmd

    nc = bacc.Bacc("TRN2", target_bir_lowering=False, num_devices=1)
    arrays = {}

    def given(name, a):
        a = np.ascontiguousarray(a)
        arrays["in_" + name] = a
        return nc.dram_tensor("in_" + name, a.shape, mybir.dt.from_np(a.dtype), kind="ExternalInput").ap()

    def halves(w, b=None, rows=P):
        out = np.zeros((rows, 2, w.shape[1]), np.float32)
        out[:CH] = w.reshape(2, CH, -1).transpose(1, 0, 2)
        if b is not None:
            out[CH, 1] = b
        return out

    row = np.arange(P) % N
    heads = np.stack([(row // HD == h) & (row < HG * HD) for h in range(HG)], 1).astype(np.float32)
    causal = np.where(np.arange(N)[None, :] > row[:, None], np.float32(MASKED), np.float32(0))
    gains = np.zeros((P, 4), np.float32)
    for i, name in enumerate(("qn_g", "qn_b", "kn_g", "kn_b")):
        for grp in range(QG):
            for h in range(HG):
                r = N * grp + HD * h
                gains[r:r + HD, i] = inputs["L0_cond_" + name]
    const = np.concatenate([np.eye(P, dtype=np.float32), causal, heads, gains, np.zeros((P, HG), np.float32)], 1)

    order = np.arange(C).reshape(SETS, QG, HG * HD).transpose(1, 0, 2).ravel()
    w_d = []
    for l in range(2):
        p = {k[len("Lx_cond_"):]: np.asarray(a) for k, a in inputs.items() if k.startswith(f"L{l}_cond_")}
        if l == 0:
            ada, qkv = halves(p["w_ada"], p["b_ada"], KR), halves(p["w_qkv"], p["b_qkv"])
            proj, w1_, w2_, b2_ = halves(p["w_proj"][order], p["b_proj"]), halves(p["w1"], p["b1"]), p["w2"], p["b2"]
        else:
            ada, qkv = halves(p["Wa"], p["ba"], KR), halves(np.concatenate([p["Wq"], p["Wk"], p["Wv"]], 1))
            proj, w1_, w2_, b2_ = halves(p["Wp"][order], p["bp"]), halves(p["W1"], p["b1"]), p["W2"], p["b2"]
        down = np.zeros((FM * P, C), np.float32)
        down[:F], down[F] = w2_, b2_
        w_d.append([given(f"ada{l}", ada), given(f"qkv{l}", qkv), given(f"pw1_{l}", np.concatenate([proj, w1_], 2)),
                    given(f"down{l}", down.reshape(FM, P, C).transpose(1, 0, 2))])
    x = given("x", inputs["x"]).rearrange("(t j) n c -> (j n) t c", j=SEQ)
    c = given("c", inputs["cond_1152"])
    out = nc.dram_tensor("out", (B, N, C), F32, kind="ExternalOutput").ap()
    build(nc, x, c, given("const", const), w_d, out.rearrange("(t j) n c -> t (j n) c", j=SEQ))
    r = run_bass_kernel_spmd(nc, [arrays], core_ids=[0])
    return r.results[0]["out"]
```

```python
from contextlib import ExitStack

import concourse.bass as bass
from concourse import mybir

F32 = mybir.dt.float32
F32R = mybir.dt.float32r
BF16 = mybir.dt.bfloat16
I32 = mybir.dt.int32
ALU = mybir.AluOpType
ACT = mybir.ActivationFunctionType
AX = mybir.AxisListType.X

B, N, C = 32, 32, 144
H, HD = 16, 9
F = 4 * C
P = 128
SEQ = P // N
T = B // SEQ
CH = C // 2
KR = CH + 1
KH = [CH, KR]
Q3 = 3 * C
M6 = 6 * C
PARTS = 3
QG, HG = 4, 2
SETS = H // (QG * HG)
GH = 4
G = H // GH
VW = HD + 1
REST = C - P
UPPER = -4096
FM = (F + P - 1) // P
FP = FM * P
UP = 2 * C
FR = F - (FM - 1) * P
STEPS = range(-2, 2 * T + 3)
SPLITS = (1, 2, T - 2)
EPS_X, EPS_QK = 1e-6, 1e-5
MAGIC = float(0x5F3759DF)
RS_OPS = 8
RS_SCALE = 64 / 9
VQ, VX1, VX2 = slice(0, 2 * H), 2 * H, 2 * H + 1
VN = 2 * H + 2
MASKED = -1e30
ZERO = 13 + GH


def build(nc, x_d, c_d, const_d, w_d, out_d):
    with ExitStack() as ctx:
        def sb(name, shape, dt=F32):
            return ctx.enter_context(nc.sbuf_tensor(name, shape, dt))

        def bank(name):
            return ctx.enter_context(nc.psum_tensor(name, [P, 512], F32))

        def sem(name):
            return ctx.enter_context(nc.semaphore(name))

        const = sb("const", [P, P + N + HG + 4])
        ident = const[:, 0:P]
        mask_f = const[:, P:P + N]
        head_cols = const[:, P + N:P + N + HG]
        qk_gain = const[:, P + N + HG:P + N + HG + 4].rearrange("p (i b) -> p i b", i=2)
        ident_bf = sb("ident_bf", [P, P], BF16)
        mask_bf = sb("mask_bf", [P, N], BF16)
        wada = [sb(f"wada{l}", [KR, 2, M6]) for l in range(2)]
        wqkv = [sb(f"wqkv{l}", [P, 2, Q3]) for l in range(2)]
        wpw1 = [sb(f"wpw1_{l}", [P, UP + 2 * FP]) for l in range(2)]
        w2 = [sb(f"w2_{l}", [P, FM, C]) for l in range(2)]
        last_rows = [wqkv[0][:, 1, :], wpw1[0][:, UP + FP:], wqkv[1][:, 1, :], wpw1[1][:, UP + FP:]]
        upper_w = sb("upper_w", [P, 4, FP])
        parts_w = [sb(f"parts_w{k}", [P, w.shape[1]], F32R) for k, w in enumerate(last_rows)]
        head_mean = sb("head_mean", [P, 2, 2 * H])
        cond = sb("cond", [B, C])
        cond_t = sb("cond_t", [KR, 2, B])
        cond_t0 = sb("cond_t0", [KR, 2, P])
        mod = sb("mod", [B, 2, M6])
        modb = [sb(f"modb{l}", [P, T, M6]) for l in range(2)]
        q_aff = sb("q_aff", [P, 2, 2])
        k_aff = sb("k_aff", [P, 2, HG, 2])
        x = sb("x", [P, T, C])
        stats = sb("stats", [P, 2, 6])
        mv = sb("mv", [P, 2, 2])
        var = sb("var", [P, VN])
        rs = sb("rs", [P, VN])
        rw = sb("rw", [P, 2, VN])
        xc = sb("xc", [P, C])
        xn = sb("xn", [P, 2, P])
        rest = sb("rest", [P, REST])
        xt, xt_rest = sb("xt", [P, P]), sb("xt_rest", [P, P], F32R)
        v = sb("v", [P, T, C])
        vblk = sb("vblk", [P, SEQ, G, GH, VW])
        sq = sb("sq", [P, 2 * C])
        ssum = sb("ssum", [P, 2 * H])
        qkn = sb("qkn", [P, 2 * SETS * QG, N])
        qt = sb("qt", [P, SETS, P])
        kblk = sb("kblk", [P, SETS, HG, P])
        ahead = sb("ahead", [P, 1])
        smax = sb("smax", [P, H])
        prob = sb("prob", [P, H, N])
        prob_t = sb("prob_t", [P, G, P])
        srec = sb("srec", [P, H])
        o = sb("o", [P, C])
        ot = sb("ot", [P, 2, P])
        y = sb("y", [P, C])
        xc2 = sb("xc2", [P, C])
        xn2 = sb("xn2", [P, 2, P])
        rest2 = sb("rest2", [P, REST])
        xt2, xt2_rest = sb("xt2", [P, P]), sb("xt2_rest", [P, P], F32R)
        ht = sb("ht", [P, FM, P])
        y2 = sb("y2", [P, C])

        ps_t = bank("ps_t")
        ps_q = bank("ps_q")
        ps_s = ctx.enter_context(nc.psum_tensor("ps_s", [P, QG, 512], F32))
        sv = ps_s[:, :, 0:GH * N]
        ps_pt = bank("ps_pt")
        ps_o = bank("ps_o")

        s_const, s_cond, s_x0, s_x = sem("s_const"), sem("s_cond"), sem("s_x0"), sem("s_x")
        s_wada = [sem("s_wada0"), sem("s_wada1")]
        s_wqkv = [sem("s_wqkv0"), sem("s_wqkv1")]
        s_w = [sem("s_w0"), sem("s_w1")]
        s_zero = sem("s_zero")
        s_chain = sem("s_chain")
        s_set = sem("s_set")
        s_cent = sem("s_cent")
        s_upper, s_split = sem("s_upper"), sem("s_split")
        s_silu, s_ct, s_ctc = sem("s_silu"), sem("s_ct"), sem("s_ctc")
        s_mod0, s_mods0 = sem("s_mod0"), sem("s_mods0")
        s_mod, s_mods = sem("s_mod"), sem("s_mods")
        s_modd = [sem(f"s_modd{k}") for k in range(3)]
        s_modb = [[sem(f"s_modb{l}_{k}") for k in range(2)] for l in range(2)]
        s_bn1, s_bn2, s_mv1, s_mv2 = sem("s_bn1"), sem("s_bn2"), sem("s_mv1"), sem("s_mv2")
        s_ssum, s_vq = sem("s_ssum"), sem("s_vq")
        s_vx, s_rs = sem("s_vx"), sem("s_rs")
        s_xc1, s_xn, s_xnt, s_xt = sem("s_xc1"), sem("s_xn"), sem("s_xnt"), sem("s_xt")
        s_qkv, s_sq, s_v, s_vcopy, s_vblk = sem("s_qkv"), sem("s_sq"), sem("s_v"), sem("s_vcopy"), sem("s_vblk")
        s_qkn, s_qkt, s_kblk = sem("s_qkn"), sem("s_qkt"), sem("s_kblk")
        s_table = sem("s_table")
        s_s0, s_s, s_exp = sem("s_s0"), sem("s_s"), sem("s_exp")
        s_max, s_sub = sem("s_max"), sem("s_sub")
        s_pt, s_ptc, s_o, s_rec, s_on = sem("s_pt"), sem("s_ptc"), sem("s_o"), sem("s_rec"), sem("s_on")
        s_ott, s_ot, s_proj, s_gate, s_res = sem("s_ott"), sem("s_ot"), sem("s_proj"), sem("s_gate"), sem("s_res")
        s_rest1, s_rest2 = sem("s_rest1"), sem("s_rest2")
        s_xc2, s_xn2, s_x2t, s_xt2 = sem("s_xc2"), sem("s_xn2"), sem("s_x2t"), sem("s_xt2")
        s_h5, s_h, s_ht5, s_ht = sem("s_h5"), sem("s_h"), sem("s_ht5"), sem("s_ht")
        s_y, s_out = sem("s_y"), sem("s_out")
        s_gate2, s_res2 = sem("s_gate2"), sem("s_res2")

        scratch = nc.dram_tensor("mod_scratch", (2, B, M6), F32).ap()

        def pipeline(eng, step, ahead, behind):
            n = STEPS.start
            for l in range(2):
                for g in range(n, T * l + behind):
                    step(0, g)
                with eng.Fori(behind, T - ahead) as r:
                    step(l, r)
                n = T * (l + 1) - ahead
            for g in range(n, STEPS.stop + 1):
                step(0, g)

        def pair(l, n, k):
            if isinstance(n, int):
                g = T * l + n + k
                return 0 <= g < 2 * T, g // T, g % T, g
            return True, l, n + k, T * l + n + k

        def wait_past(eng, s, count):
            if not isinstance(count, int) or count > 0:
                eng.wait_ge(s, count)

        def tile(buf, t, a=0, b=C):
            return buf[:, bass.ds(t, 1), a:b].rearrange("p a c -> p (a c)")

        def parts(k, ops, s):
            up = upper_w[:, k, 0:last_rows[k].shape[1]]
            ops.tensor_copy(parts_w[k][0:P // 2, :], up[0:P // 2, :]).then_inc(s, 1)
            return ops.tensor_tensor(parts_w[k][P // 2:P, :], last_rows[k][P // 2:P, :], up[P // 2:P, :], ALU.subtract)

        block = ctx.enter_context(nc.Block())

        @block.sync
        def _(sp):
            sp.dma_start(cond[:], c_d).then_inc(s_cond, 16)
            sp.dma_start(const[:], const_d).then_inc(s_const, 16)
            sp.dma_start(wada[0][:], w_d[0][0]).then_inc(s_wada[0], 16)
            sp.dma_start(x[:, 0, :], x_d[:, 0, :]).then_inc(s_x0, 16)
            sp.dma_start(wqkv[0][:], w_d[0][1]).then_inc(s_wqkv[0], 16)
            sp.dma_start(x[:, 1:T, :], x_d[:, 1:T, :]).then_inc(s_x, 16)
            sp.dma_start(wada[1][:], w_d[1][0]).then_inc(s_wada[1], 16)

            def spread(l, k, first_tile):
                cols = [slice(0, 2 * C), slice(2 * C, M6)][k]
                for j in range(SEQ):
                    src = scratch[l, SEQ * first_tile + j::SEQ, cols].rearrange("(a t) m -> a t m", a=1).broadcast_to(
                        [N, T - first_tile, cols.stop - cols.start])
                    sp.dma_start(modb[l][N * j:N * j + N, first_tile:T, cols], src).then_inc(s_modb[l][k], 16)

            sp.wait_ge(s_mods, 2)
            sp.dma_start(scratch[0, :, 0:2 * C], mod[:, 0, 0:2 * C]).then_inc(s_modd[0], 16)
            sp.wait_ge(s_modd[0], 16)
            spread(0, 0, 1)
            sp.dma_start(wpw1[0][:], w_d[0][2]).then_inc(s_w[0], 16)
            sp.wait_ge(s_mods, 2 * PARTS)
            sp.dma_start(scratch[0, :, 2 * C:M6], mod[:, 0, 2 * C:M6]).then_inc(s_modd[1], 16)
            sp.dma_start(w2[0][:], w_d[0][3]).then_inc(s_w[0], 16)
            sp.wait_ge(s_modd[1], 16)
            spread(0, 1, 0)
            sp.dma_start(wqkv[1][:], w_d[1][1]).then_inc(s_wqkv[1], 16)
            sp.dma_start(wpw1[1][:], w_d[1][2]).then_inc(s_w[1], 16)
            sp.dma_start(w2[1][:], w_d[1][3]).then_inc(s_w[1], 16)
            sp.wait_ge(s_mods, 4 * PARTS)
            sp.dma_start(scratch[1], mod[:, 1, :]).then_inc(s_modd[2], 16)
            sp.wait_ge(s_modd[2], 16)
            spread(1, 0, 0)
            spread(1, 1, 0)
            for t in range(T):
                sp.wait_ge(s_res2, T + t + 2)
                sp.dma_start(out_d[t], x[:, t, :]).then_inc(s_out, 16)
            sp.wait_ge(s_out, 16 * T)

        @block.gpsimd
        def _(pool):
            gp = nc.gpsimd
            gp.memset(ahead[:], 0.0).then_inc(s_zero, 1)
            gp.memset(cond_t[:], 1.0).then_inc(s_zero, 1)
            gp.memset(cond_t0[:], 1.0).then_inc(s_zero, 1)
            gp.memset(xn[:], 0.0).then_inc(s_zero, 1)
            gp.memset(xn2[:], 0.0).then_inc(s_zero, 1)
            gp.memset(ot[:], 1.0).then_inc(s_zero, 1)
            gp.memset(ht[:, FM - 1, :], 1.0).then_inc(s_zero, 1)
            gp.memset(qkn[:], 0.0).then_inc(s_zero, 1)
            gp.memset(var[:], 1.0).then_inc(s_zero, 1)
            gp.memset(mv[:], 1.0).then_inc(s_zero, 1)
            gp.memset(vblk[:], 0.0).then_inc(s_zero, 1)
            pool.wait_ge(s_zero, 11)
            for h in range(GH):
                gp.memset(vblk[N * h:N * h + N, :, :, h, HD:VW], 1.0).then_inc(s_zero, 1)
            pool.wait_ge(s_zero, ZERO - 2)
            for out in (xn, xn2):
                gp.memset(out[:, 1, :].rearrange("p (i j c) -> p i j c", i=2, j=2)[:, :, 0, REST:REST + 1], 1.0).then_inc(s_zero, 1)
            pool.wait_ge(s_zero, ZERO)
            gp.memset(y2[:], 0.0).then_inc(s_res2, 1)
            pool.wait_ge(s_res2, 1)

            def split(k):
                pool.wait_ge(s_upper, k)
                parts(k, gp, s_split).then_inc(s_split, 1)
                pool.wait_ge(s_split, 2 * k)

            def step(l, n):
                ok, _, t, g = pair(l, n, 0)
                if ok:
                    pool.wait_ge(s_v, g + 1)
                    wait_past(pool, s_o, g)
                    for h in range(GH):
                        for j in range(SEQ):
                            last = gp.tensor_copy(
                                vblk[N * h:N * h + N, j, :, h, 0:HD],
                                v[N * j:N * j + N, bass.ds(t, 1), :].rearrange("p a (s g h c) -> p (a s) g h c", s=SETS, g=G, h=HG)
                                [:, h // HG, :, h % HG, :])
                        if h < GH - 1:
                            last.then_inc(s_vcopy, 1)
                            pool.wait_ge(s_vcopy, (GH - 1) * g + h + 1)
                    last.then_inc(s_vblk, 1)
                    pool.wait_ge(s_vblk, g + 1)
                ok, _, t, g = pair(l, n, -1)
                if ok:
                    pool.wait_ge(s_gate, g + 1)
                    gp.tensor_tensor(tile(x, t), tile(x, t), y[:], ALU.add).then_inc(s_res, 1)
                    pool.wait_ge(s_res, g + 1)
                ok, _, t, g = pair(l, n, -3)
                if ok:
                    pool.wait_ge(s_gate2, g + 2)
                    gp.tensor_tensor(tile(x, t), tile(x, t), y2[:], ALU.add).then_inc(s_res2, 1)
                    pool.wait_ge(s_res2, g + 2)

                if isinstance(n, int) and n in SPLITS:
                    split(SPLITS.index(n) + 1)

            pipeline(pool, step, 2, 3)

        @block.scalar
        def _(act):
            a = nc.scalar
            act.wait_ge(s_cond, 16)
            a.activation(cond[:], cond[:], ACT.Silu).then_inc(s_silu, 1)
            act.wait_ge(s_zero, ZERO)
            act.wait_ge(s_ct, 1)
            ct = ps_t[0:CH, 0:2 * B].rearrange("p (h t) -> p h t", h=2)
            for half in range(2):
                a.copy(cond_t0[0:CH, half, :].rearrange("p (j n) -> p j n", j=SEQ),
                       ct[:, half, 0:SEQ].unsqueeze(2).broadcast_to([CH, SEQ, N])).then_inc(s_ctc, 1)
            a.copy(cond_t[0:CH], ct).then_inc(s_ctc, 1)
            act.wait_ge(s_set, 1)

            def step(l, n):
                ok, b, t, g = pair(l, n, -4)
                if ok:
                    func = ACT.Silu if b else ACT.Gelu
                    act.wait_ge(s_h5, g + 1)
                    a.activation(ht[0:FR, FM - 1, :], ps_pt[0:FR, 0:P], func).then_inc(s_ht5, 1)
                    act.wait_ge(s_h, g + 1)
                    a.activation(ht[:, 0:FM - 1, :], sv, func).then_inc(s_ht, 1)
                ok, b, t, g = pair(l, n, 0)
                if ok:
                    act.wait_ge(s_qkt, g + 1)
                    wait_past(act, s_s, g)
                    a.activation(qt[:], ps_pt[:, 0:SETS * P].rearrange("p (s t) -> p s t", s=SETS), ACT.Identity,
                                 scale=q_aff[:, b, 0:1], bias=q_aff[:, b, 1:2])
                ok, b, t, g = pair(l, n, 1)
                if ok:
                    act.wait_ge(s_xnt, g + 1)
                    a.copy(xt[:], ps_t[:, 0:P])
                    a.copy(xt_rest[:], ps_t[:, P:2 * P]).then_inc(s_xt, 1)
                ok, b, t, g = pair(l, n, 0)
                if ok:
                    for h in range(HG):
                        last = a.activation(kblk[:, :, h, :], ps_pt[:, SETS * P:2 * SETS * P].rearrange("p (s t) -> p s t", s=SETS),
                                            ACT.Identity, scale=k_aff[:, b, h, 0:1], bias=k_aff[:, b, h, 1:2])
                    last.then_inc(s_kblk, 1)
                ok, b, t, g = pair(l, n, 1)
                if ok:
                    act.wait_ge(s_qkv, g + 1)
                    if b == 0:
                        wait_past(act, s_vq, g)
                        a.activation(sq[:], ps_q[:, 0:2 * C], ACT.Square).then_inc(s_sq, 1)
                    a.copy(v[:, bass.ds(t, 1), :], ps_q[:, 2 * C:3 * C].unsqueeze(1)).then_inc(s_v, 1)
                ok, b, t, g = pair(l, n, -1)
                if ok:
                    act.wait_ge(s_pt, g + 1)
                    a.copy(prob_t[:], ps_pt[:].rearrange("p (g t) -> p g t", g=G)).then_inc(s_ptc, 1)
                ok, b, t, g = pair(l, n, 0)
                if ok:
                    wait_past(act, s_table, g)
                    a.activation(ahead[:], ahead[:], ACT.Exp, scale=0.0).then_inc(s_table, 1)
                ok, b, t, g = pair(l, n, -3)
                if ok:
                    act.wait_ge(s_x2t, g + 1)
                    a.copy(xt2[:], ps_t[:, 0:P])
                    a.copy(xt2_rest[:], ps_t[:, P:2 * P]).then_inc(s_xt2, 1)
                ok, b, t, g = pair(l, n, 0)
                if ok:
                    act.wait_ge(s_sub, 2 * g + 2)
                    a.activation(prob[:], prob[:], ACT.Exp).then_inc(s_exp, 1)

            pipeline(act, step, 1, 4)

        @block.vector
        def _(dve):
            d = nc.vector
            links = [0]

            def link(ins):
                links[0] += 1
                ins.then_inc(s_chain, 1)
                dve.wait_ge(s_chain, links[0])

            def take(out, ps, part, done):
                for i in range(2):
                    cols = slice(i * C, i * C + C)
                    if (part, i) in ((0, 1), (2, 0)):
                        last = d.tensor_scalar(out[:, cols], ps[:, cols], 1.0, None, ALU.add)
                    else:
                        last = d.tensor_copy(out[:, cols], ps[:, cols])
                    last.then_inc(done, 1)

            def modulation(l, part, ps):
                dve.wait_ge(s_mod, PARTS * l + part + 1)
                take(mod[:, l, part * 2 * C:(part + 1) * 2 * C], ps[0:B, 0:2 * C], part, s_mods)

            dve.wait_ge(s_const, 16)
            link(d.tensor_copy(ident_bf[:], ident))
            link(d.tensor_copy(mask_bf[:], mask_f))
            link(d.tensor_scalar(q_aff[:, 0, :], qk_gain[:, 0, :], HD ** -0.5, None, ALU.mult))
            link(d.memset(q_aff[:, 1, :], 0.0))
            link(d.memset(q_aff[:, 1, 0:1], HD ** -0.5))
            link(d.memset(k_aff[:, 1], 0.0))
            for h in range(HG):
                link(d.tensor_scalar(k_aff[:, 0, h, :], qk_gain[:, 1, :], head_cols[:, h:h + 1], None, ALU.mult))
                link(d.tensor_copy(k_aff[:, 1, h, 0:1], head_cols[:, h:h + 1]))
            dve.wait_ge(s_zero, ZERO)
            d.memset(smax[:], 0.0).then_inc(s_set, 1)
            d.memset(rw[:], 0.0).then_inc(s_gate2, 1)

            def centre():
                w = wqkv[0][:, :, 0:2 * C].rearrange("p i (g c) -> p i g c", c=HD)
                dve.wait_ge(s_wqkv[0], 16)
                link(d.tensor_reduce(head_mean[:], w, AX, ALU.add))
                link(d.tensor_scalar(head_mean[:], head_mean[:], 1.0 / HD, None, ALU.mult))
                d.tensor_tensor(w, w, head_mean[:].unsqueeze(3).broadcast_to([P, 2, 2 * H, HD]), ALU.subtract).then_inc(s_cent, 1)
                dve.wait_ge(s_cent, 1)
                link(upper_part(0))
                parts(0, d, s_cent).then_inc(s_cent, 1)

            def upper_part(k):
                return d.tensor_scalar(upper_w[:, k, 0:last_rows[k].shape[1]].bitcast(I32), last_rows[k].bitcast(I32), UPPER, None,
                                       ALU.bitwise_and)

            def modulated(out, x_scaled, root, shift, rest, s, g):
                groups = out[:, 1, :].rearrange("p (i j c) -> p i j c", i=2, j=2)
                up, low = groups[:, :, 0, 0:REST], groups[:, :, 1, 0:REST]
                twice = rest[:].unsqueeze(1).broadcast_to([P, 2, REST])
                d.scalar_tensor_tensor(rest[:], x_scaled[:, P:C], root, shift[:, P:C], ALU.mult, ALU.add).then_inc(s, 1)
                d.scalar_tensor_tensor(out[:, 0, :], x_scaled[:, 0:P], root, shift[:, 0:P], ALU.mult, ALU.add)
                dve.wait_ge(s, 2 * g + 1)
                d.tensor_scalar(up.bitcast(I32), twice.bitcast(I32), UPPER, None, ALU.bitwise_and).then_inc(s, 1)
                dve.wait_ge(s, 2 * g + 2)
                return d.tensor_tensor(low, twice, up, ALU.subtract)

            def rsqrt(cols, s, base, first, stop):
                y, v, u, z = rs[:, cols], var[:, cols], rw[:, 0, cols], rw[:, 1, cols]
                for k in range(first, stop):
                    if k > 0:
                        dve.wait_ge(s, base + k)
                    if k == 0:
                        ins = d.tensor_scalar(y.bitcast(I32), v.bitcast(I32), -0.5, MAGIC, ALU.mult, ALU.add)
                    elif k == 1:
                        ins = d.tensor_tensor(u, y, y, ALU.mult)
                    elif k == 2 or k == 6:
                        ins = d.tensor_tensor(u, u, v, ALU.mult)
                    elif k == 3:
                        ins = d.scalar_tensor_tensor(u, u, -10 / 3, u, ALU.add, ALU.mult)
                    elif k == 4:
                        ins = d.scalar_tensor_tensor(z, u, 5.0, y, ALU.add, ALU.mult)
                    elif k == 5:
                        ins = d.scalar_tensor_tensor(u, z, -9 / 128, z, ALU.mult, ALU.mult)
                    else:
                        ins = d.scalar_tensor_tensor(y, u, 1.5, z, ALU.add, ALU.mult)
                    ins.then_inc(s, 1)

            def step(l, n):
                step_no = (T * l + n) - STEPS.start
                late, front, mid, back, prior, mlp = [pair(l, n, k) for k in (2, 1, 0, -1, -2, -4)]
                ok1, b1, t1, g1 = late
                ok2, b2, t2, g2 = prior
                if ok1:
                    if b1 == 1:
                        dve.wait_ge(s_res2, g1 - T + 2)
                    d.bn_stats(stats[:, 0, :], tile(x, t1)).then_inc(s_bn1, 1)
                if ok2:
                    dve.wait_ge(s_res, g2 + 1)
                    d.bn_stats(stats[:, 1, :], tile(x, t2)).then_inc(s_bn2, 1)
                ok, b, t, g = mlp
                if ok:
                    dve.wait_ge(s_y, g + 1)
                    dve.wait_ge(s_res2, g + 1)
                    d.tensor_tensor(y2[:], ps_o[:, 0:C], tile(modb[b], t, 5 * C, 6 * C), ALU.mult).then_inc(s_gate2, 1)
                if ok1:
                    dve.wait_ge(s_bn1, g1 + 1)
                if ok2:
                    dve.wait_ge(s_bn2, g2 + 1)
                if ok1 or ok2:
                    d.memset(rw[:, 0, VX1:VN], 0.0)
                if ok1:
                    d.bn_aggr(mv[:, 0, :], stats[:, 0, :]).then_inc(s_mv1, 1)
                if ok2:
                    d.bn_aggr(mv[:, 1, :], stats[:, 1, :]).then_inc(s_mv2, 1)
                if ok1:
                    dve.wait_ge(s_mv1, g1 + 1)
                if ok2:
                    dve.wait_ge(s_mv2, g2 + 1)
                if ok1 or ok2:
                    d.tensor_scalar(var[:, VX1:VN], mv[:, :, 1], EPS_X, RS_SCALE, ALU.add, ALU.mult).then_inc(s_vx, 1)
                ok, b, t, g = front
                norm = ok and b == 0
                if norm:
                    dve.wait_ge(s_sq, g + 1)
                    d.tensor_reduce(ssum[:], sq[:].rearrange("p (g c) -> p g c", c=HD), AX, ALU.add).then_inc(s_ssum, 1)
                    dve.wait_ge(s_ssum, g + 1)
                    d.tensor_scalar(var[:, VQ], ssum[:], RS_SCALE / HD, RS_SCALE * EPS_QK, ALU.mult, ALU.add).then_inc(s_vq, 1)
                    dve.wait_ge(s_vq, g + 1)
                roots = norm or ok1 or ok2
                root = slice(0 if norm else VX1, VN), s_rs, RS_OPS * step_no
                if ok1 or ok2:
                    dve.wait_ge(s_vx, step_no + 1)
                if roots:
                    rsqrt(*root, 0, 2)
                def less_max(half, link):
                    ok, b, t, g = mid
                    scores = sv[:, half * 2:half * 2 + 2, :].rearrange("p g (h k) -> p g h k", k=N)
                    m = smax[:, half * H // 2:(half + 1) * H // 2].rearrange("p (g h) -> p g h", g=2)
                    if ok:
                        dve.wait_ge([s_s0, s_s][half], g + 1)
                        d.tensor_reduce(m, scores, AX, ALU.max).then_inc(s_max, 1)
                    if roots:
                        rsqrt(*root, link, link + 1)
                    if ok:
                        dve.wait_ge(s_max, 2 * g + half + 1)
                        if half == 0:
                            wait_past(dve, s_pt, g)
                        d.tensor_tensor(prob[:, half * H // 2:(half + 1) * H // 2, :].rearrange("p (g h) k -> p g h k", g=2),
                                        scores, m.unsqueeze(3).broadcast_to([P, 2, GH, N]), ALU.subtract).then_inc(s_sub, 1)

                less_max(0, 2)
                less_max(1, 3)
                ok, b, t, g = back
                ov = ps_o[:, 0:H * VW].rearrange("p (h c) -> p h c", c=VW)
                if ok:
                    dve.wait_ge(s_o, g + 1)
                    d.reciprocal(srec[:], ov[:, :, HD]).then_inc(s_rec, 1)
                if roots:
                    rsqrt(*root, 4, 5)
                if ok:
                    dve.wait_ge(s_rec, g + 1)
                    wait_past(dve, s_ott, g)
                    d.tensor_tensor(o[:].rearrange("p (h c) -> p h c", c=HD), ov[:, :, 0:HD],
                                    srec[:].unsqueeze(2).broadcast_to([P, H, HD]), ALU.mult).then_inc(s_on, 1)
                if roots:
                    rsqrt(*root, 5, 6)
                if isinstance(n, int) and n == -2:
                    dve.wait_ge(s_mod0, 1)
                    take(modb[0][:, 0, 0:2 * C], ps_q[:, 0:2 * C], 0, s_mods0)
                    dve.wait_ge(s_mods0, 2)
                if isinstance(n, int) and n == -1:
                    dve.wait_ge(s_modb[0][0], 16 * SEQ)
                if ok1:
                    d.scalar_tensor_tensor(xc[:], tile(x, t1), mv[:, 0, 0:1], tile(modb[b1], t1, C, 2 * C),
                                           ALU.subtract, ALU.mult).then_inc(s_xc1, 1)
                if roots:
                    rsqrt(*root, 6, 7)
                if ok2:
                    d.scalar_tensor_tensor(xc2[:], tile(x, t2), mv[:, 1, 0:1], tile(modb[b2], t2, 4 * C, 5 * C),
                                           ALU.subtract, ALU.mult).then_inc(s_xc2, 1)
                ok, b, t, g = back
                if ok:
                    dve.wait_ge(s_ott, g + 1)
                    d.tensor_copy(ot[0:CH], ps_t[0:CH, 0:2 * P].rearrange("p (h t) -> p h t", h=2)).then_inc(s_ot, 1)
                if roots:
                    rsqrt(*root, 7, 8)
                    dve.wait_ge(s_rs, RS_OPS * (step_no + 1))
                ok, b, t, g = front
                if ok:
                    dve.wait_ge(s_v, g + 1)
                    wait_past(dve, s_qkt, g)
                    if b == 0:
                        d.tensor_tensor(
                            qkn[:, :, 0:HG * HD].rearrange("p b (h c) -> p b h c", h=HG),
                            ps_q[:, 0:2 * C].rearrange("p (b h c) -> p b h c", h=HG, c=HD),
                            rs[:, VQ].rearrange("p (b h) -> p b h", h=HG).unsqueeze(3).broadcast_to([P, 2 * SETS * QG, HG, HD]),
                            ALU.mult).then_inc(s_qkn, 1)
                    else:
                        d.tensor_copy(qkn[:, :, 0:HG * HD], ps_q[:, 0:2 * C].rearrange("p (b c) -> p b c", c=HG * HD))\
                         .then_inc(s_qkn, 1)
                if ok1:
                    dve.wait_ge(s_xc1, g1 + 1)
                    wait_past(dve, s_xnt, g1)
                    modulated(xn, xc, rs[:, VX1:VX1 + 1], tile(modb[b1], t1, 0, C), rest, s_rest1, g1).then_inc(s_xn, 1)
                ok, b, t, g = back
                if ok:
                    dve.wait_ge(s_proj, g + 1)
                    wait_past(dve, s_res, g)
                    d.tensor_tensor(y[:], ps_o[:, 0:C], tile(modb[b], t, 2 * C, 3 * C), ALU.mult).then_inc(s_gate, 1)
                if isinstance(n, int) and n == -1:
                    modulation(0, 2, ps_s[:, 2, :])
                    modulation(1, 0, ps_s[:, 3, :])
                if isinstance(n, int) and n in (1, 2):
                    modulation(1, n, ps_s[:, 0, :])
                if isinstance(n, int) and n in SPLITS:
                    k = SPLITS.index(n) + 1
                    dve.wait_ge(*[(s_w[0], 32), (s_wqkv[1], 16), (s_w[1], 32)][k - 1])
                    upper_part(k).then_inc(s_upper, 1)
                if ok2:
                    dve.wait_ge(s_xc2, g2 + 1)
                    wait_past(dve, s_x2t, g2)
                    modulated(xn2, xc2, rs[:, VX2:VX2 + 1], tile(modb[b2], t2, 3 * C, 4 * C), rest2, s_rest2, g2)\
                        .then_inc(s_xn2, 1)

            def step_with_loads(l, n):
                if isinstance(n, int) and n == -2:
                    dve.wait_ge(s_x0, 16)
                if isinstance(n, int) and n == -1:
                    modulation(0, 0, ps_s[:, 0, :])
                    centre()
                    modulation(0, 1, ps_s[:, 1, :])
                    dve.wait_ge(s_x, 16)
                if isinstance(n, int) and n == 1:
                    dve.wait_ge(s_modb[0][1], 16 * SEQ)
                if isinstance(n, int) and n == T - 2:
                    dve.wait_ge(s_modb[1][0], 16 * SEQ)
                    dve.wait_ge(s_modb[1][1], 16 * SEQ)
                step(l, n)

            pipeline(dve, step_with_loads, 2, 4)

        @block.tensor
        def _(pe):
            mm, tr = nc.tensor.matmul, nc.tensor.transpose

            def modulation(l, part, cond_rows, out, done):
                for half in range(2):
                    last = mm(out, cond_rows[0:KH[half], half, :], wada[l][0:KH[half], half, part * 2 * C:(part + 1) * 2 * C],
                              start=half == 0, stop=half == 1)
                last.then_inc(done, 1)

            def transpose_halves(src, done):
                for half in range(2):
                    last = tr(ps_t[0:CH, half * P:half * P + P], src[:, half * CH:half * CH + CH], ident)
                last.then_inc(done, 1)

            def transpose_blocks(src, done):
                for part in range(2):
                    last = tr(ps_t[:, part * P:part * P + P], src[:, part, :], ident)
                last.then_inc(done, 1)

            def product(out, lhs, rhs, lhs_rest, rhs_rest):
                mm(out, lhs, rhs, start=True, stop=False)
                return mm(out, lhs_rest, rhs_rest, start=False, stop=True)

            pe.wait_ge(s_silu, 1)
            pe.wait_ge(s_const, 16)
            for half in range(2):
                last = tr(ps_t[0:CH, half * B:half * B + B], cond[:, half * CH:half * CH + CH], ident[0:B, 0:B])
            last.then_inc(s_ct, 1)
            pe.wait_ge(s_wada[0], 16)
            pe.wait_ge(s_ctc, 3)
            modulation(0, 0, cond_t0, ps_q[:, 0:2 * C], s_mod0)
            for part in range(2):
                modulation(0, part, cond_t, ps_s[0:B, part, 0:2 * C], s_mod)

            def step(l, n):
                if isinstance(n, int) and n == -1:
                    pe.wait_ge(s_mods0, 2)
                    pe.wait_ge(s_cent, 3)
                if isinstance(n, int) and n == T - 1:
                    pe.wait_ge(s_split, 4)
                    pe.wait_ge(s_wqkv[1], 16)
                    pe.wait_ge(s_w[1], 32)
                if isinstance(n, int) and T * l + n == T + 2:
                    pe.wait_ge(s_split, 6)
                late, front, mid, back, mlp = [pair(l, n, k) for k in (2, 1, 0, -1, -3)]
                ok, b, t, g = front
                if ok:
                    pe.wait_ge(s_xt, g + 1)
                    product(ps_q[:, 0:Q3], xt[:], wqkv[b][:, 0, :], xt_rest[:], parts_w[2 * b][:]).then_inc(s_qkv, 1)
                if isinstance(n, int) and n == -1:
                    modulation(0, 2, cond_t, ps_s[0:B, 2, 0:2 * C], s_mod)
                    pe.wait_ge(s_wada[1], 16)
                    modulation(1, 0, cond_t, ps_s[0:B, 3, 0:2 * C], s_mod)
                if isinstance(n, int) and n == 0:
                    pe.wait_ge(s_mods, 2 * (PARTS + 1))
                if isinstance(n, int) and n == 1:
                    pe.wait_ge(s_w[0], 32)
                ok, b, t, g = mid
                if ok:
                    pe.wait_ge(s_kblk, g + 1)
                ok, b, t, g = back
                if ok:
                    pe.wait_ge(s_exp, g + 1)
                    for grp in range(G):
                        last = tr(ps_pt[:, grp * P:grp * P + P], prob[:, grp * GH:(grp + 1) * GH, :].rearrange("p h k -> p (h k)"),
                                  ident)
                    last.then_inc(s_pt, 1)
                ok, b, t, g = mid
                if ok:
                    for half in range(2):
                        groups = range(half * QG // 2, (half + 1) * QG // 2)
                        if b == 1:
                            for i in groups:
                                mm(ps_s[:, i, 0:GH * N], ident_bf[:], mask_bf[:].unsqueeze(1).broadcast_to([P, GH, N]),
                                   start=True, stop=False, skip_group_check=True)
                        for s in range(SETS):
                            for j in range(SEQ):
                                for i in groups:
                                    rows = slice(N * i, N * i + N)
                                    last = mm(ps_s[N * j:N * j + N, i, s * HG * N:(s + 1) * HG * N], qt[rows, s, N * j:N * j + N],
                                              kblk[rows, s, :, N * j:N * j + N], start=b == 0, stop=True, skip_group_check=b == 1)
                        if half == 0:
                            last.then_inc(s_s0, 1)
                    last.then_inc(s_s, 1)
                ok, b, t, g = mlp
                if ok:
                    pe.wait_ge(s_xn2, g + 1)
                    transpose_blocks(xn2, s_x2t)
                ok, b, t, g = back
                if ok:
                    wait_past(pe, s_gate, g)
                    wait_past(pe, s_gate2, g - 1)
                    pe.wait_ge(s_vblk, g + 1)
                    pe.wait_ge(s_ptc, g + 1)
                    for j in range(SEQ):
                        for grp in range(G):
                            last = mm(ps_o[N * j:N * j + N, grp * GH * VW:(grp + 1) * GH * VW], prob_t[:, grp, N * j:N * j + N],
                                      vblk[:, j, grp, :, :].rearrange("p h c -> p (h c)"), start=True, stop=True)
                    last.then_inc(s_o, 1)

                def up(m):
                    out = ps_s[:, m, 0:P] if m < FM - 1 else ps_pt[:, 0:P]
                    return product(out, wpw1[b][:, UP + m * P:UP + (m + 1) * P], xt2[:],
                                   parts_w[2 * b + 1][:, m * P:(m + 1) * P], xt2_rest[:])

                ok, b, t, g = mlp
                if ok:
                    pe.wait_ge(s_xt2, g + 1)
                    up(FM - 1).then_inc(s_h5, 1)
                    pe.wait_ge(s_sub, min(2 * g + 8, 4 * T) if isinstance(n, int) else 2 * g + 8)
                    up(0)
                if back[0]:
                    pe.wait_ge(s_on, back[3] + 1)
                    transpose_halves(o, s_ott)
                if isinstance(n, int) and n in (1, 2):
                    pe.wait_ge(s_sub, 2 * n + 2)
                    modulation(1, n, cond_t, ps_s[0:B, 0, 0:2 * C], s_mod)
                if ok:
                    for m in range(1, FM - 1):
                        last = up(m)
                    last.then_inc(s_h, 1)
                ok, b, t, g = back
                if ok:
                    pe.wait_ge(s_ot, g + 1)
                    for half in range(2):
                        last = mm(ps_o[:, 0:C], ot[:, half, :], wpw1[b][:, half * C:half * C + C], start=half == 0, stop=half == 1)
                    last.then_inc(s_proj, 1)
                ok, b, t, g = front
                if ok:
                    if mlp[0]:
                        pe.wait_ge(s_ht5, g - 3)
                    pe.wait_ge(s_qkn, g + 1)
                    for k in range(2 * SETS):
                        last = tr(ps_pt[:, k * P:k * P + P], qkn[:, k * QG:(k + 1) * QG, :].rearrange("p b c -> p (b c)"), ident)
                    last.then_inc(s_qkt, 1)
                ok, b, t, g = late
                if ok:
                    pe.wait_ge(s_xn, g + 1)
                    transpose_blocks(xn, s_xnt)
                ok, b, t, g = mlp
                if ok:
                    pe.wait_ge(s_gate, min(g + 3, 2 * T) if isinstance(n, int) else g + 3)
                    if not back[0]:
                        pe.wait_ge(s_gate2, g + 1)
                    pe.wait_ge(s_ht, g + 1)
                    for m in range(FM):
                        rows = P if m < FM - 1 else FR + 1
                        last = mm(ps_o[:, 0:C], ht[0:rows, m, :], w2[b][0:rows, m, :], start=m == 0, stop=m == FM - 1)
                    last.then_inc(s_y, 1)
                if isinstance(n, int) and n in (1, 2):
                    pe.wait_ge(s_mods, 2 * (PARTS + n + 1))
                if isinstance(n, int) and n == 2:
                    pe.wait_ge(s_split, 2)

            pipeline(pe, step, 2, 3)


def kernel(**inputs):
    import numpy as np
    import concourse.bacc as bacc
    from concourse import mybir
    from concourse.bass_utils import run_bass_kernel_spmd

    nc = bacc.Bacc("TRN2", target_bir_lowering=False, num_devices=1)
    arrays = {}

    def given(name, a):
        a = np.ascontiguousarray(a)
        arrays["in_" + name] = a
        return nc.dram_tensor("in_" + name, a.shape, mybir.dt.from_np(a.dtype), kind="ExternalInput").ap()

    def halves(w, b=None, rows=P):
        out = np.zeros((rows, 2, w.shape[1]), np.float32)
        out[:CH] = w.reshape(2, CH, -1).transpose(1, 0, 2)
        if b is not None:
            out[CH, 1] = b
        return out

    def split_rows(w, b=None, cols=0):
        out = np.zeros((P, 2, cols or w.shape[1]), np.float32)
        out[:, 0, :w.shape[1]] = w[:P]
        for r0 in range(0, P, N):
            out[r0:r0 + REST, 1, :w.shape[1]] = w[P:]
            if b is not None:
                out[r0 + REST, 1, :w.shape[1]] = b
        return out

    row = np.arange(P) % N
    heads = np.stack([(row // HD == h) & (row < HG * HD) for h in range(HG)], 1).astype(np.float32)
    causal = np.where(np.arange(N)[None, :] > row[:, None], np.float32(MASKED), np.float32(0))
    gains = np.zeros((P, 4), np.float32)
    for i, name in enumerate(("qn_g", "qn_b", "kn_g", "kn_b")):
        for grp in range(QG):
            for h in range(HG):
                r = N * grp + HD * h
                gains[r:r + HD, i] = inputs["L0_cond_" + name]
    const = np.concatenate([np.eye(P, dtype=np.float32), causal, heads, gains], 1)

    order = np.arange(C).reshape(SETS, QG, HG * HD).transpose(1, 0, 2).ravel()
    w_d = []
    for l in range(2):
        p = {k[len("Lx_cond_"):]: np.asarray(a) for k, a in inputs.items() if k.startswith(f"L{l}_cond_")}
        if l == 0:
            ada, qkv = halves(p["w_ada"], p["b_ada"], KR), split_rows(p["w_qkv"], p["b_qkv"])
            proj, w1_, w2_, b2_ = halves(p["w_proj"][order], p["b_proj"]), split_rows(p["w1"], p["b1"], FP), p["w2"], p["b2"]
        else:
            ada, qkv = halves(p["Wa"], p["ba"], KR), split_rows(np.concatenate([p["Wq"], p["Wk"], p["Wv"]], 1))
            proj, w1_, w2_, b2_ = halves(p["Wp"][order], p["bp"]), split_rows(p["W1"], p["b1"], FP), p["W2"], p["b2"]
        down = np.zeros((FM * P, C), np.float32)
        down[:F], down[F] = w2_, b2_
        w_d.append([given(f"ada{l}", ada), given(f"qkv{l}", qkv),
                    given(f"pw1_{l}", np.concatenate([proj.reshape(P, -1), w1_.reshape(P, -1)], 1)),
                    given(f"down{l}", down.reshape(FM, P, C).transpose(1, 0, 2))])
    x = given("x", inputs["x"]).rearrange("(t j) n c -> (j n) t c", j=SEQ)
    c = given("c", inputs["cond_1152"])
    out = nc.dram_tensor("out", (B, N, C), F32, kind="ExternalOutput").ap()
    build(nc, x, c, given("const", const), w_d, out.rearrange("(t j) n c -> t (j n) c", j=SEQ))
    r = run_bass_kernel_spmd(nc, [arrays], core_ids=[0])
    return r.results[0]["out"]
```
